# Optimizing a Trainium2 kernel written in Bass

```python
import numpy as np
import jax
import jax.numpy as jnp

def _softmax(x, axis=-1):
    return jax.nn.softmax(x, axis=axis)

def _gelu(x):
    return jax.nn.gelu(x, approximate=True)

def _silu(x):
    return jax.nn.silu(x)

def _sigmoid(x):
    return jax.nn.sigmoid(x)

def _layernorm(x, axis=-1, eps=1e-05):
    m = jnp.mean(x, axis=axis, keepdims=True)
    v = jnp.var(x, axis=axis, keepdims=True)
    return (x - m) / jnp.sqrt(v + eps)

def _scatter_add(tgt, idx, src, axis=0):
    return tgt.at[idx].add(src)

def _segment_sum(src, seg, n):
    return jax.ops.segment_sum(src, seg, n)
kernel_name = 'mk_gnn_preln_d2_gnn_r8_03b80a'

def setup_inputs(seed: int=0):
    np.random.seed(seed)
    _w = jnp.asarray

    def _rec_inputs():
        import jax
        import jax.numpy as jnp
        _gk = jax.random.key(seed)
        x = -0.0003713 + 1 * jax.random.normal(jax.random.fold_in(_gk, 1), (6250, 256), jnp.float32)
        src = jax.random.randint(jax.random.fold_in(_gk, 2), (200000,), 0, 6250, jnp.int32)
        dst = jnp.minimum((6250 * jax.random.uniform(jax.random.fold_in(_gk, 3), (200000,)) ** 2.0).astype(jnp.int32), 49999)
        _o = jnp.argsort(dst, stable=True)
        src = src[_o]
        dst = dst[_o]
        edge_attr_16 = 0.000196303 + 1.00016 * jax.random.normal(jax.random.fold_in(_gk, 11), (200000, 16), jnp.float32)
        edge_type_8 = jax.random.randint(jax.random.fold_in(_gk, 13), (200000,), 0, 8, jnp.int32)
        return (x, src, dst, edge_attr_16, edge_type_8)
    x, src, dst, edge_attr_16, edge_type_8 = _rec_inputs()

    def _L0_gnn_setup():
        import jax, jax.numpy as jnp
        import numpy as np
        N_NODES = 6250
        key = jax.random.key(seed)
        ks = jax.random.split(key, 6)
        d_in, d_out = (256, 256)
        n_edges = 200000
        x = jax.random.normal(ks[0], (N_NODES, d_in), dtype=jnp.float32)
        edge_index = jax.random.randint(ks[1], (2, n_edges), 0, N_NODES, dtype=jnp.int64)
        edge_attr = jax.random.normal(ks[2], (n_edges, 16), dtype=jnp.float32)
        W1 = jax.random.normal(ks[3], (d_in, d_out), dtype=jnp.float32) * (1.0 / np.sqrt(d_in))
        b1 = jnp.zeros((d_out,), dtype=jnp.float32)
        W2 = jax.random.normal(ks[4], (d_out, d_out), dtype=jnp.float32) * (1.0 / np.sqrt(d_out))
        b2 = jnp.zeros((d_out,), dtype=jnp.float32)
        eps = jnp.zeros((1,), dtype=jnp.float32)
        return {'x': x, 'edge_index': edge_index, 'edge_attr': edge_attr, 'W1': W1, 'b1': b1, 'W2': W2, 'b2': b2, 'eps': eps}
    _L0_gnn_all = _L0_gnn_setup()
    _L0_gnn_in = {k: v for k, v in _L0_gnn_all.items() if k in ('W1', 'b1', 'W2', 'b2', 'eps')}
    del _L0_gnn_all

    def _L1_gnn_setup():
        import jax, jax.numpy as jnp
        import numpy as np
        N_NODES = 6250
        N_EDGES = 100000
        IN_FEAT = 256
        OUT_FEAT = 256
        NUM_RELS = 8
        ALPHA = 0.5
        key = jax.random.key(seed)
        k1, k2, k3, k4, k5, k6 = jax.random.split(key, 6)
        x = jax.random.normal(k1, (N_NODES, IN_FEAT), dtype=jnp.float32)
        edge_index = jax.random.randint(k2, (2, N_EDGES), 0, N_NODES, dtype=jnp.int64)
        edge_type = jax.random.randint(k3, (N_EDGES,), 0, NUM_RELS, dtype=jnp.int64)
        gain = float(np.sqrt(2.0))
        lim_w = gain * float(np.sqrt(6.0 / (IN_FEAT + OUT_FEAT)))
        weight = jax.random.uniform(k4, (NUM_RELS, IN_FEAT, OUT_FEAT), dtype=jnp.float32, minval=-lim_w, maxval=lim_w)
        loop_weight = jax.random.uniform(k5, (IN_FEAT, OUT_FEAT), dtype=jnp.float32, minval=-lim_w, maxval=lim_w)
        h_bias = jnp.zeros((OUT_FEAT,), dtype=jnp.float32)
        return {'edge_index': edge_index, 'x': x, 'edge_type': edge_type, 'weight': weight, 'h_bias': h_bias, 'loop_weight': loop_weight}
    _L1_gnn_all = _L1_gnn_setup()
    _L1_gnn_in = {k: v for k, v in _L1_gnn_all.items() if k in ('weight', 'h_bias', 'loop_weight')}
    del _L1_gnn_all
    return {'x': x, 'src': src, 'dst': dst, 'edge_attr_16': edge_attr_16, 'edge_type_8': edge_type_8, 'L0_gnn_W1': _L0_gnn_in['W1'], 'L0_gnn_b1': _L0_gnn_in['b1'], 'L0_gnn_W2': _L0_gnn_in['W2'], 'L0_gnn_b2': _L0_gnn_in['b2'], 'L0_gnn_eps': _L0_gnn_in['eps'], 'L1_gnn_weight': _L1_gnn_in['weight'], 'L1_gnn_h_bias': _L1_gnn_in['h_bias'], 'L1_gnn_loop_weight': _L1_gnn_in['loop_weight']}

def reference(x, src, dst, edge_attr_16, edge_type_8, L0_gnn_W1, L0_gnn_b1, L0_gnn_W2, L0_gnn_b2, L0_gnn_eps, L1_gnn_weight, L1_gnn_h_bias, L1_gnn_loop_weight):
    import jax
    import jax.numpy as jnp

    def _L0_gnn_ref(x, edge_index, edge_attr, W1, b1, W2, b2, eps):
        import jax, jax.numpy as jnp
        import numpy as np
        N_NODES = 6250
        src, dst = (edge_index[0], edge_index[1])
        agg = jax.ops.segment_sum(x[src], dst, num_segments=N_NODES)
        h = (1.0 + eps[0]) * x + agg
        h = jax.nn.relu(h @ W1 + b1)
        out = h @ W2 + b2
        return out

    def _L1_gnn_ref(edge_index, x, edge_type, weight, h_bias, loop_weight):
        import jax, jax.numpy as jnp
        import numpy as np
        N_NODES = 6250
        N_EDGES = 100000
        IN_FEAT = 256
        OUT_FEAT = 256
        NUM_RELS = 8
        ALPHA = 0.5
        num_nodes = x.shape[0]
        src, dst = (edge_index[0], edge_index[1])
        hx = jnp.einsum('ni,rio->rno', x, weight)
        msg = hx[edge_type, src]
        agg = jax.ops.segment_sum(msg, dst, num_segments=num_nodes)
        node_repr = agg * jnp.asarray(ALPHA, x.dtype) ** 0.5
        node_repr = node_repr + h_bias
        loop_message = x @ loop_weight
        node_repr = node_repr + loop_message * jnp.asarray(1.0 - ALPHA, x.dtype) ** 0.5
        return node_repr
    edge_index = jnp.stack([src, dst])
    h = jnp.maximum(_layernorm(x, axis=-1), 0.0)
    x = x + _L0_gnn_ref(h, edge_index, edge_attr_16, L0_gnn_W1, L0_gnn_b1, L0_gnn_W2, L0_gnn_b2, L0_gnn_eps)
    h = jnp.maximum(_layernorm(x, axis=-1), 0.0)
    x = x + _L1_gnn_ref(edge_index, h, edge_type_8, L1_gnn_weight, L1_gnn_h_bias, L1_gnn_loop_weight)
    return x

_drawn_inputs = setup_inputs


def setup_inputs(seed=0):
    import zlib

    import numpy as np

    out = dict(_drawn_inputs(seed))
    spreads = {'L0_gnn_b1': (0.0, 0.8), 'L0_gnn_b2': (0.0, 0.753), 'L1_gnn_h_bias': (0.0, 0.8)}
    factors = {}
    for name, (base, spread) in spreads.items():
        noise = np.random.default_rng([zlib.crc32(name.encode()), seed]).standard_normal(out[name].shape)
        drawn = base * np.exp(spread * noise) if base else spread * noise
        out[name] = jnp.asarray(drawn.astype(out[name].dtype))
    for name, factor in factors.items():
        out[name] = (out[name] * factor).astype(out[name].dtype)
    return out
```

```python
import concourse.bass as bass
from concourse import mybir
from contextlib import ExitStack

F32 = mybir.dt.float32
I32 = mybir.dt.int32
ALU = mybir.AluOpType
ACT = mybir.ActivationFunctionType
AX = mybir.AxisListType


def later(n, least):
    return not isinstance(n, int) or n >= least


def gnn_program(nc, x, src, dst, edge_type, W1, b1, W2, b2, eps, Wrel, rel_bias, Wloop, out):
    N, D = x.shape
    E, = src.shape
    R = Wrel.shape[0]
    P = 128
    C = D // P
    KT = 8
    GE = KT * P
    NG = -(-E // GE)
    TAIL = E - (NG - 1) * GE
    TAIL_P = TAIL // KT
    NB = 2
    GB = NG // NB
    SLOTS = 4
    ROUNDS = NG // SLOTS
    W = P
    NT = -(-N // P)
    LAST = N - P
    OVER = (NT - 1) * P - LAST
    ACC = N + W
    ST = 4
    SETS = (NT - 1) // ST
    PAIRS = SETS // 2
    FREE_BANKS = 2
    NCONST = 9
    NOWHERE = 1 << 14
    HALF = 0.5 ** 0.5
    LN_EPS = 1e-5
    NCH = R * D // 512
    RC = 512 // D
    assert NG == NB * GB and NG == SLOTS * ROUNDS and TAIL % KT == 0 and (NT - 1) % (2 * ST) == 0
    assert NOWHERE > N + W and NCH == 4 and C == 2

    h0_rows = nc.dram_tensor("h0_rows", (N, D), F32, kind="Internal").ap()
    msg_rows = nc.dram_tensor("msg_rows", (N, R * D), F32, kind="Internal").ap()
    msg_table = msg_rows.rearrange("n (r d) -> (n r) d", r=R)
    rest_rows = nc.dram_tensor("rest_rows", (N, D), F32, kind="Internal").ap()

    with ExitStack() as ctx:
        def sb(name, shape, dt=F32):
            return ctx.enter_context(nc.sbuf_tensor(name, shape, dt))

        def sem(name):
            return ctx.enter_context(nc.semaphore(name))

        sums = sb("sums", [P, C, ACC])
        rows = sb("rows", [P, SLOTS, KT, D])
        onehot = sb("onehot", [P, 2, KT, W])
        idx_all = sb("idx_all", [P, 2, NG, KT], I32)
        idx = sb("idx", [P, SLOTS, KT], I32)
        dst_all = sb("dst_all", [P, NG, KT])
        local = sb("local", [P, NG + 1, KT])
        base_f = sb("base_f", [P, NG])
        base_i = sb("base_i", [P, NG], I32)
        check = sb("check", [P, 4])
        in_windows = sb("in_windows", [P, 1], I32)
        iota_i = sb("iota_i", [P, W], I32)
        iota_w = sb("iota_w", [P, W])
        window = sb("window", [P, W])
        part_i = sb("part_i", [P, 1], I32)
        part_f = sb("part_f", [P, 1])
        ident = sb("ident", [P, P])
        first = sb("first", [P, P])
        w1 = sb("w1", [P, C, D])
        w2 = sb("w2", [P, C, D])
        wrel = sb("wrel", [P, C, R, D])
        wloop = sb("wloop", [P, C, D])
        b1_c = sb("b1_c", [P, C])
        b2_r = sb("b2_r", [P, D])
        bias_r = sb("bias_r", [P, D])
        eps1 = sb("eps1", [P, 1])
        lneps = sb("lneps", [P, 1])
        xin = sb("xin", [P, 2, ST, D])
        h_out = sb("h_out", [P, 2, ST, D])
        stats = sb("stats", [P, 2, ST, 6])
        meanvar = sb("meanvar", [P, 2, ST, 2])
        std = sb("std", [P, 2, ST])
        rstd = sb("rstd", [P, 2, ST])
        shift = sb("shift", [P, 2, ST])
        hidden = sb("hidden", [P, 2, C, P])
        x1 = sb("x1", [P, 2, D])
        h1t = sb("h1t", [P, 2, C, P])
        msg = sb("msg", [P, 2, R * D])
        room = [rows[:, n].rearrange("p k (b f) -> p (k b f)", b=1) for n in range(SLOTS)]

        def as_blocks(ap):
            return ap.rearrange("p (b e) -> p b e", b=NB)

        src_raw, type_raw, dst_raw = (as_blocks(room[n].bitcast(I32)) for n in (0, 1, 2))
        src_f, type_f, to_msg_f, dst_f = (as_blocks(room[n]) for n in (3, 0, 1, 0))
        final = msg[:, :, 0:C * ST * P].rearrange("p s (c n) -> p s c n", c=C)

        psum = ctx.enter_context(nc.psum_tensor("psum", [P, 8, 512], F32))
        bank = [psum[:, n] for n in range(8)]

        s_pad = sem("s_pad")
        s_lists = sem("s_lists")
        s_float = sem("s_float")
        s_const = sem("s_const")
        s_iota = sem("s_iota")
        s_ident = sem("s_ident")
        s_weights = sem("s_weights")
        s_eps_in = sem("s_eps_in")
        s_eps = sem("s_eps")
        s_listT = sem("s_listT")
        s_listC = sem("s_listC")
        s_base = sem("s_base")
        s_base_c = sem("s_base_c")
        s_local = sem("s_local")
        s_viol = sem("s_viol")
        s_max = sem("s_max")
        s_maxT = sem("s_maxT")
        s_flag = sem("s_flag")
        s_xin = [sem(f"s_xin{n}") for n in range(2)]
        s_stats = sem("s_stats")
        s_mv = sem("s_mv")
        s_std = sem("s_std")
        s_rstd = sem("s_rstd")
        s_shift = sem("s_shift")
        s_h0 = sem("s_h0")
        s_h0t = sem("s_h0t")
        s_self = sem("s_self")
        s_h0st = [sem(f"s_h0st{n}") for n in range(2)]
        s_free = [sem(f"s_free{n}") for n in range(SLOTS)]
        s_idx = [sem(f"s_idx{n}") for n in range(SLOTS)]
        s_rows = [sem(f"s_rows{n}") for n in range(SLOTS)]
        s_onehot = sem("s_onehot")
        s_group = sem("s_group")
        s_added = sem("s_added")
        s_window = sem("s_window")
        s_sums = sem("s_sums")
        s_zero = sem("s_zero")
        s_x3 = [sem(f"s_x3{n}") for n in range(2)]
        s_y1 = sem("s_y1")
        s_hid = sem("s_hid")
        s_y2 = sem("s_y2")
        s_xb = sem("s_xb")
        s_x1 = sem("s_x1")
        s_x1b = sem("s_x1b")
        s_stats3 = sem("s_stats3")
        s_mv3 = sem("s_mv3")
        s_std3 = sem("s_std3")
        s_rstd3 = sem("s_rstd3")
        s_shift3 = sem("s_shift3")
        s_h1 = sem("s_h1")
        s_h1tp = sem("s_h1tp")
        s_h1t = sem("s_h1t")
        s_msg = [sem(f"s_msg{n}") for n in range(NCH)]
        s_msgc = [sem(f"s_msgc{n}") for n in range(NCH)]
        s_loop = sem("s_loop")
        s_rest = sem("s_rest")
        s_msgst = [sem(f"s_msgst{n}") for n in range(2)]
        s_restst = [sem(f"s_restst{n}") for n in range(2)]
        s_rin = [sem(f"s_rin{n}") for n in range(2)]
        s_fin = sem("s_fin")
        s_fint = sem("s_fint")
        s_out = sem("s_out")
        s_outst = [sem(f"s_outst{n}") for n in range(2)]
        s_pass = {e: sem(f"s_pass_{e}") for e in ("pool", "act", "dve")}

        set_rows = "(t p) d -> p t d"
        block = ctx.enter_context(nc.Block())

        def set_of(rows_ap, n):
            return rows_ap[bass.ds(n * ST * P, ST * P), :].rearrange(set_rows, p=P)

        @block.sync
        def _(sp):
            for n in range(2):
                sp.dma_start(xin[:, n], set_of(x, n)).then_inc(s_xin[n], 16)
            for to, of in ((eps1[:], eps.partition_broadcast(P)), (b2_r[:], b2.partition_broadcast(P)),
                           (bias_r[:], rel_bias.partition_broadcast(P)),
                           (w1[:], W1.rearrange("(k p) d -> p k d", p=P)),
                           (w2[:], W2.rearrange("(k p) d -> p k d", p=P)),
                           (wloop[:], Wloop.rearrange("(k p) d -> p k d", p=P)),
                           (wrel[:, 0], Wrel[:, 0:P].rearrange("r p d -> p r d")),
                           (wrel[:, 1], Wrel[:, P:D].rearrange("r p d -> p r d"))):
                sp.dma_start(to, of).then_inc(s_weights, 16)
            sp.dma_start(b1_c[:], b1.rearrange("(o p) -> p o", p=P), allow_slow_non_contiguous=True
                         ).then_inc(s_weights, 16)
            sp.wait_ge(s_pad, 1)
            for raw, flat in ((src_raw, src), (type_raw, edge_type), (dst_raw, dst)):
                g = 0
                for b, m in ((0, GB), (1, GB - 2), (1, 1)):
                    p0 = g - GB * b
                    sp.dma_start(raw[p0:p0 + m, b, :],
                                 flat[g * GE:(g + m) * GE].rearrange("(g e) -> g e", e=GE)).then_inc(s_lists, 16)
                    g += m
                sp.dma_start(raw[GB - 1:GB, 1, 0:TAIL],
                             flat[(NG - 1) * GE:E].rearrange("(g e) -> g e", g=1)).then_inc(s_lists, 16)

            def h0_set(i, n, s, tiles, then):
                sp.wait_ge(s_h0, n + 1)
                if tiles == ST:
                    sp.dma_start(set_of(h0_rows, n), h_out[:, s]).then_inc(s_h0st[s], 16)
                else:
                    sp.dma_start(h0_rows[LAST + OVER:N, :], h_out[OVER:P, s, 0]).then_inc(s_h0st[s], 16)
                if then == ST:
                    sp.dma_start(xin[:, s], set_of(x, n + 2)).then_inc(s_xin[s], 16)
                elif then:
                    sp.dma_start(xin[:, s, 0], x[LAST:N, :]).then_inc(s_xin[s], 16)

            with sp.Fori(0, PAIRS - 1) as i:
                for s in range(2):
                    h0_set(i, 2 * i + s, s, ST, ST)
            h0_set(PAIRS - 1, SETS - 2, 0, ST, 1)
            h0_set(PAIRS - 1, SETS - 1, 1, ST, 0)
            h0_set(PAIRS, SETS, 0, 1, 0)

            def tile_x(j, s, at):
                sp.dma_start(xin[:, s, 0], x[at:at + P, :] if isinstance(at, int) else x[bass.ds(at, P), :]
                             ).then_inc(s_x3[s], 16)

            def tile_out(j, s, at, skip=0):
                here = (lambda a: a[at + skip:at + P, :]) if isinstance(at, int) else (
                    lambda a: a[bass.ds(at, P), :])
                for n in range(NCH):
                    sp.wait_ge(s_msgc[n], j + 1)
                sp.dma_start(here(msg_rows), msg[skip:P, s]).then_inc(s_msgst[s], 16)
                sp.wait_ge(s_rest, j + 1)
                sp.dma_start(here(rest_rows), xin[skip:P, s, 3]).then_inc(s_restst[s], 16)

            sp.wait_ge(s_h0t, SETS + 1)
            tile_x(0, 0, 0)
            sp.wait_ge(s_xb, 1)
            tile_x(1, 1, P)
            with sp.Fori(0, (NT - 3) // 2) as i:
                for s in range(2):
                    sp.wait_ge(s_xb, 2 * i + s + 2)
                    tile_x(2 * i + s + 2, s, (2 * i + s + 2) * P)
                    tile_out(2 * i + s, s, (2 * i + s) * P)
            sp.wait_ge(s_xb, NT - 1)
            tile_x(NT - 1, 0, LAST)
            tile_out(NT - 3, 0, (NT - 3) * P)
            tile_out(NT - 2, 1, (NT - 2) * P)
            tile_out(NT - 1, 0, LAST, OVER)

            def out_set(n, s, tiles, then):
                sp.wait_ge(s_out, n + 1)
                if tiles == ST:
                    sp.dma_start(set_of(out, n), h_out[:, s]).then_inc(s_outst[s], 16)
                else:
                    sp.dma_start(out[LAST + OVER:N, :], h_out[OVER:P, s, 0]).then_inc(s_outst[s], 16)
                if then == ST:
                    sp.dma_start(xin[:, s], set_of(rest_rows, n + 2)).then_inc(s_rin[s], 16)
                elif then:
                    sp.dma_start(xin[:, s, 0], rest_rows[LAST:N, :]).then_inc(s_rin[s], 16)

            sp.wait_ge(s_restst[0], 16 * (NT + 1) // 2)
            sp.wait_ge(s_restst[1], 16 * (NT // 2))
            for n in range(2):
                sp.dma_start(xin[:, n], set_of(rest_rows, n)).then_inc(s_rin[n], 16)
            with sp.Fori(0, PAIRS - 1) as i:
                for s in range(2):
                    out_set(2 * i + s, s, ST, ST)
            out_set(SETS - 2, 0, ST, 1)
            out_set(SETS - 1, 1, ST, 0)
            out_set(SETS, 0, 1, 0)
            sp.wait_ge(s_outst[0], 16 * (PAIRS + 1))
            sp.wait_ge(s_outst[1], 16 * PAIRS)

        @block.gpsimd
        def _(pool):
            nc.gpsimd.iota(iota_i[:], pattern=[[1, W]], base=0, channel_multiplier=0)
            nc.gpsimd.iota(part_i[:], pattern=[[0, 1]], base=0, channel_multiplier=1).then_inc(s_const, 1)
            nc.gpsimd.memset(src_raw, 0)
            nc.gpsimd.memset(type_raw, 0)
            nc.gpsimd.memset(dst_raw, NOWHERE).then_inc(s_pad, 1)
            pool.wait_ge(s_lists, 16 * 12)
            nc.gpsimd.tensor_copy(src_f, src_raw).then_inc(s_float, 1)
            pool.wait_ge(s_float, 1)
            nc.gpsimd.tensor_copy(type_f, type_raw).then_inc(s_float, 1)
            pool.wait_ge(s_float, 2)
            nc.gpsimd.tensor_scalar(to_msg_f, src_f, float(R), None, ALU.mult).then_inc(s_float, 1)
            pool.wait_ge(s_float, 3)
            nc.gpsimd.tensor_tensor(to_msg_f, to_msg_f, type_f, ALU.add).then_inc(s_float, 1)
            pool.wait_ge(s_float, 4)
            nc.gpsimd.tensor_copy(dst_f, dst_raw).then_inc(s_float, 1)

            def gather(layer, table):
                with pool.Fori(0, ROUNDS) as i:
                    for b in range(SLOTS):
                        pool.wait_ge(s_idx[b], i + (layer * ROUNDS + 1))
                        pool.sem_inc(s_pass["pool"], 1)
                        for k in range(KT):
                            pool.indirect_dma_start(
                                out=rows[:, b, k], out_offset=None, in_=table,
                                in_offset=bass.IndirectOffsetOnAxis(ap=idx[:, b, k:k + 1], axis=0),
                            ).then_inc(s_rows[b], 16)

            pool.wait_ge(s_h0st[0], 16 * (PAIRS + 1))
            pool.wait_ge(s_h0st[1], 16 * PAIRS)
            gather(0, h0_rows)
            pool.wait_ge(s_y1, NT)
            nc.gpsimd.memset(sums[:], 0.0).then_inc(s_zero, 1)
            pool.wait_ge(s_msgst[0], 16 * (NT + 1) // 2)
            pool.wait_ge(s_msgst[1], 16 * (NT // 2))
            gather(1, msg_table)

        @block.scalar
        def _(act):
            def h0_set(i, n, s, tiles):
                act.wait_ge(s_mv, n + 1)
                nc.scalar.activation(std[:, s, 0:tiles], meanvar[:, s, 0:tiles, 1], ACT.Sqrt,
                                     bias=lneps[:]).then_inc(s_std, 1)
                act.wait_ge(s_shift, n + 1)
                if later(n, 2):
                    act.wait_ge(s_h0t, n - 1)
                    act.wait_ge(s_h0st[s], 16 * i)
                for t in range(tiles):
                    last = nc.scalar.activation(h_out[:, s, t], xin[:, s, t], ACT.Relu,
                                                bias=shift[:, s, t:t + 1], scale=rstd[:, s, t:t + 1])
                last.then_inc(s_h0, 1)

            act.wait_ge(s_iota, 1)
            for s in range(2):
                h0_set(0, s, s, ST)
            with act.Fori(1, PAIRS) as i:
                for s in range(2):
                    h0_set(i, 2 * i + s, s, ST)
            h0_set(PAIRS, SETS, 0, 1)

            for n in range(3 * NB * 2):
                a, b, h = n // (NB * 2), n // 2 % NB, n % 2
                act.wait_ge(s_listT, n + 1)
                to = idx_all[:, a] if a < 2 else dst_all[:]
                nc.scalar.copy(to[:, b * GB:(b + 1) * GB, 4 * h:4 * h + 4].rearrange("p g k -> p k g"),
                               bank[4 + n % 4][:, 0:4 * GB].rearrange("p (k g) -> p k g", k=4)
                               ).then_inc(s_listC, 1)
            act.wait_ge(s_listC, 12)

            def feed(layer):
                with act.Fori(0, ROUNDS) as i:
                    for b in range(SLOTS):
                        act.wait_ge(s_free[b], i + (layer * ROUNDS + 1))
                        act.sem_inc(s_pass["act"], 1)
                        nc.scalar.copy(idx[:, b], idx_all[:, layer, bass.ds(SLOTS * i + b, 1), :].rearrange(
                            "p g k -> p (g k)")).then_inc(s_idx[b], 1)

            feed(0)
            act.wait_ge(s_weights, 16 * NCONST)

            def front(j, s):
                act.wait_ge(s_y1, j + 1)
                if later(j, 2):
                    act.wait_ge(s_y2, j - 1)
                for o in range(C):
                    last = nc.scalar.activation(hidden[:, s, o], bank[4][:, o * P:(o + 1) * P], ACT.Relu,
                                                bias=b1_c[:, o:o + 1])
                last.then_inc(s_hid, 1)

            def norm(j, s):
                act.wait_ge(s_mv3, j + 1)
                nc.scalar.activation(std[:, s, 0:1], meanvar[:, s, 0, 1:2], ACT.Sqrt,
                                     bias=lneps[:]).then_inc(s_std3, 1)
                act.wait_ge(s_shift3, j + 1)
                if later(j, 2):
                    act.wait_ge(s_h1tp, j - 1)
                nc.scalar.activation(h_out[:, s, 0], x1[:, s], ACT.Relu,
                                     bias=shift[:, s, 0:1], scale=rstd[:, s, 0:1]).then_inc(s_h1, 1)

            def turned(j, s):
                act.wait_ge(s_h1tp, j + 1)
                if later(j, 2):
                    act.wait_ge(s_loop, j - 1)
                nc.scalar.copy(h1t[:, s], bank[6][:, 0:C * P].rearrange("p (c n) -> p c n", c=C)
                               ).then_inc(s_h1t, 1)

            def messages(j, s, r, n):
                act.wait_ge(s_msg[n], j + 1)
                if later(r, 1):
                    act.wait_ge(s_msgst[s], 16 * r)
                nc.scalar.copy(msg[:, s, 512 * n:512 * (n + 1)], bank[n][:]).then_inc(s_msgc[n], 1)

            def step(i, j, s):
                front(j, s)
                if later(j, 1):
                    messages(j - 1, 1 - s, i - 1 + s, 0)
                norm(j, s)
                if later(j, 1):
                    messages(j - 1, 1 - s, i - 1 + s, 2)
                turned(j, s)

            for s in range(2):
                step(0, s, s)
            step(1, 2, 0)
            step(1, 3, 1)
            with act.Fori(2, NT // 2) as i:
                for s in range(2):
                    step(i, 2 * i + s, s)
            step(NT // 2, NT - 1, 0)
            messages(NT - 1, 0, NT // 2, 0)
            messages(NT - 1, 0, NT // 2, 2)

            feed(1)

            def to_turn(n, s, tiles):
                if later(n, 2):
                    act.wait_ge(s_fint, n - 1)
                    act.sem_inc(s_pass["act"], 1)
                at = n * (ST * P) if tiles == ST else LAST
                nc.scalar.copy(final[:, s, :, 0:tiles * P], sums[:, :, bass.ds(at, tiles * P)]).then_inc(s_fin, 1)

            act.wait_ge(s_sums, 2)
            for s in range(2):
                to_turn(s, s, ST)
            with act.Fori(1, PAIRS) as i:
                for s in range(2):
                    to_turn(2 * i + s, s, ST)
            to_turn(SETS, 0, 1)

        @block.vector
        def _(dve):
            def stage_in(i, n, s, tiles):
                dve.wait_ge(s_xin[s], 16 * (i + 1))
                for t in range(tiles):
                    last = nc.vector.bn_stats(stats[:, s, t], xin[:, s, t])
                last.then_inc(s_stats, 1)
                dve.wait_ge(s_stats, n + 1)
                dve.sem_inc(s_pass["dve"], 1)
                for t in range(tiles):
                    last = nc.vector.bn_aggr(meanvar[:, s, t], stats[:, s, t])
                last.then_inc(s_mv, 1)

            def stage_norm(n, s, tiles):
                dve.wait_ge(s_std, n + 1)
                nc.vector.reciprocal(rstd[:, s, 0:tiles], std[:, s, 0:tiles]).then_inc(s_rstd, 1)
                dve.wait_ge(s_rstd, n + 1)
                nc.vector.scalar_tensor_tensor(out=shift[:, s, 0:tiles], in0=meanvar[:, s, 0:tiles, 0],
                                               scalar=-1.0, in1=rstd[:, s, 0:tiles],
                                               op0=ALU.mult, op1=ALU.mult).then_inc(s_shift, 1)

            def stage_self(n, s, tiles):
                at = n * (ST * P) if tiles == ST else LAST
                dve.wait_ge(s_h0t, n + 1)
                for c in range(C):
                    last = nc.vector.tensor_scalar(sums[:, c, bass.ds(at, tiles * P)],
                                                   bank[2 * s + c][:, 0:tiles * P], eps1[:], None, ALU.mult)
                last.then_inc(s_self, 1)

            nc.vector.memset(lneps[:], LN_EPS)
            nc.vector.memset(first[:], 0.0)
            nc.vector.memset(local[:, NG], -1.0)
            nc.vector.memset(sums[:, :, N:ACC], 0.0).then_inc(s_iota, 1)
            dve.wait_ge(s_const, 1)
            nc.vector.tensor_copy(iota_w[:], iota_i[:])
            nc.vector.tensor_copy(part_f[:], part_i[:]).then_inc(s_iota, 1)
            dve.wait_ge(s_iota, 2)
            nc.vector.memset(first[0:1, :], 1.0)
            nc.vector.tensor_scalar(ident[:], iota_w[:], part_f[:], None, ALU.is_equal).then_inc(s_ident, 1)
            dve.wait_ge(s_weights, 16 * NCONST)
            nc.vector.tensor_scalar_add(eps1[:], eps1[:], 1.0).then_inc(s_eps, 1)
            dve.wait_ge(s_eps, 1)

            stage_in(0, 0, 0, ST)
            stage_norm(0, 0, ST)
            stage_in(0, 1, 1, ST)
            stage_self(0, 0, ST)
            stage_norm(1, 1, ST)
            with dve.Fori(1, PAIRS) as i:
                for s in range(2):
                    stage_in(i, 2 * i + s, s, ST)
                    stage_self(2 * i + s - 1, 1 - s, ST)
                    stage_norm(2 * i + s, s, ST)
            stage_in(PAIRS, SETS, 0, 1)
            stage_self(SETS - 1, 1, ST)
            stage_norm(SETS, 0, 1)
            stage_self(SETS, 0, 1)

            dve.wait_ge(s_base, 1)
            nc.vector.tensor_copy(base_f[:], bank[0][:, 0:NG])
            nc.vector.tensor_copy(base_i[:], bank[0][:, 0:NG]).then_inc(s_base_c, 1)
            dve.wait_ge(s_base_c, 1)
            nc.vector.tensor_tensor(local[:, 0:NG], dst_all[:], base_f[:].unsqueeze(2).broadcast_to([P, NG, KT]),
                                    ALU.subtract).then_inc(s_local, 1)
            dve.wait_ge(s_local, 1)
            mid = onehot[:, 0:2].rearrange("p q k w -> p (q k w)")[:, 0:NG * KT].rearrange("p (g k) -> p g k", k=KT)
            nc.vector.tensor_scalar(mid, local[:, 0:NG], -(W - 1) / 2, None, ALU.add).then_inc(s_viol, 1)
            dve.wait_ge(s_viol, 1)
            nc.vector.tensor_reduce(check[:, 0:1], mid[:, 0:NG - 1], axis=AX.XY, op=ALU.max,
                                    apply_absolute_value=True)
            nc.vector.tensor_reduce(check[0:TAIL_P, 2:3], mid[0:TAIL_P, NG - 1], axis=AX.X, op=ALU.max,
                                    apply_absolute_value=True).then_inc(s_viol, 1)
            dve.wait_ge(s_viol, 2)
            nc.vector.tensor_tensor(check[0:TAIL_P, 0:1], check[0:TAIL_P, 0:1], check[0:TAIL_P, 2:3],
                                    ALU.max).then_inc(s_max, 1)
            dve.wait_ge(s_maxT, 1)
            nc.vector.tensor_reduce(check[0:1, 1:2], bank[1][0:1, 0:P], axis=AX.X, op=ALU.max).then_inc(s_max, 1)
            dve.wait_ge(s_max, 2)
            nc.vector.tensor_scalar(in_windows[0:1, :], check[0:1, 1:2], W / 2, None, ALU.is_lt).then_inc(s_flag, 1)
            dve.wait_ge(s_flag, 1)
            windowed = dve.value_load(in_windows[0:1, 0:1], min_val=0, max_val=1)

            def one_hots(q, nodes, dests):
                return nc.vector.tensor_tensor(
                    onehot[:, q], nodes.unsqueeze(1).broadcast_to([P, KT, W]),
                    dests.rearrange("p g k -> p (g k)").unsqueeze(2).broadcast_to([P, KT, W]), ALU.is_equal)

            def add(q, at):
                cols = sums[:, :, bass.ds(at, W)]
                return nc.vector.tensor_tensor(cols, cols, psum[:, 2 * q:2 * q + C, 0:W], ALU.add)

            def accumulate(layer):
                with dve.If(windowed == 1):
                    done = layer * NG
                    one_hots(0, iota_w[:], local[:, 0:1, :]).then_inc(s_onehot, 1)
                    with dve.Fori(0, ROUNDS) as i:
                        for b in range(SLOTS):
                            g, q = SLOTS * i + b, b % 2
                            at = dve.value_load(base_i[0:1, bass.ds(g, 1)], min_val=0, max_val=N - 1)
                            one_hots(1 - q, iota_w[:], local[:, bass.ds(g + 1, 1), :]).then_inc(s_onehot, 1)
                            dve.wait_ge(s_group, g + (done + 1))
                            dve.sem_inc(s_free[b], 1)
                            dve.wait_ge(s_added, g + (done + FREE_BANKS))
                            add(q, at).then_inc(s_added, 1)
                    dve.wait_ge(s_added, done + NG + FREE_BANKS)
                with dve.Else():
                    done = layer * NG * NT
                    with dve.Fori(0, ROUNDS) as i:
                        for b in range(SLOTS):
                            g = SLOTS * i + b
                            nc.vector.tensor_scalar(window[:], iota_w[:], -float(W), None, ALU.add
                                                    ).then_inc(s_window, 1)
                            with dve.Fori(0, NT) as w:
                                n = g * NT + w
                                dve.wait_ge(s_window, n + g + (layer * NG * (NT + 1) + 1))
                                nc.vector.tensor_scalar(window[:], window[:], float(W), None, ALU.add
                                                        ).then_inc(s_window, 1)
                                dve.wait_ge(s_window, n + g + (layer * NG * (NT + 1) + 2))
                                one_hots(0, window[:], dst_all[:, bass.ds(g, 1), :]).then_inc(s_onehot, 1)
                                dve.wait_ge(s_group, n + (done + 1))
                                dve.wait_ge(s_added, n + (done + FREE_BANKS))
                                add(0, w * W).then_inc(s_added, 1)
                            dve.sem_inc(s_free[b], 1)
                    dve.wait_ge(s_added, done + NG * NT + FREE_BANKS)
                dve.sem_inc(s_sums, 1)

            dve.wait_ge(s_self, SETS + 1)
            dve.sem_inc(s_added, FREE_BANKS)
            accumulate(0)

            def front(i, j, s):
                dve.wait_ge(s_x3[s], 16 * (i + 1))
                nc.vector.tensor_tensor(xin[:, s, 1], xin[:, s, 0], b2_r[:], ALU.add).then_inc(s_xb, 1)

            def normed(j, s):
                dve.wait_ge(s_xb, j + 1)
                dve.wait_ge(s_y2, j + 1)
                nc.vector.tensor_tensor(x1[:, s], xin[:, s, 1], bank[5][:, 0:D], ALU.add).then_inc(s_x1, 1)
                dve.wait_ge(s_x1, j + 1)
                nc.vector.bn_stats(stats[:, s, 0], x1[:, s]).then_inc(s_stats3, 1)
                dve.wait_ge(s_stats3, j + 1)
                dve.sem_inc(s_pass["dve"], 1)
                nc.vector.bn_aggr(meanvar[:, s, 0], stats[:, s, 0]).then_inc(s_mv3, 1)
                dve.wait_ge(s_std3, j + 1)
                nc.vector.reciprocal(rstd[:, s, 0:1], std[:, s, 0:1]).then_inc(s_rstd3, 1)
                dve.wait_ge(s_rstd3, j + 1)
                nc.vector.scalar_tensor_tensor(out=shift[:, s, 0:1], in0=meanvar[:, s, 0, 0:1], scalar=-1.0,
                                               in1=rstd[:, s, 0:1], op0=ALU.mult, op1=ALU.mult
                                               ).then_inc(s_shift3, 1)

            def messages(j, s, r, n):
                dve.wait_ge(s_msg[n], j + 1)
                if later(r, 1):
                    dve.wait_ge(s_msgst[s], 16 * r)
                nc.vector.tensor_copy(msg[:, s, 512 * n:512 * (n + 1)], bank[n]).then_inc(s_msgc[n], 1)

            def rest(j, s, r):
                nc.vector.tensor_tensor(xin[:, s, 2], x1[:, s], bias_r[:], ALU.add).then_inc(s_x1b, 1)
                dve.wait_ge(s_x1b, j + 1)
                dve.wait_ge(s_loop, j + 1)
                if later(r, 1):
                    dve.wait_ge(s_restst[s], 16 * r)
                nc.vector.scalar_tensor_tensor(out=xin[:, s, 3], in0=bank[7][:, 0:D], scalar=HALF,
                                               in1=xin[:, s, 2], op0=ALU.mult, op1=ALU.add).then_inc(s_rest, 1)

            def step(i, j, s):
                front(i, j, s)
                if later(j, 1):
                    messages(j - 1, 1 - s, i - 1 + s, 1)
                normed(j, s)
                if later(j, 1):
                    messages(j - 1, 1 - s, i - 1 + s, 3)
                    rest(j - 1, 1 - s, i - 1 + s)

            for i in range(2):
                for s in range(2):
                    step(i, 2 * i + s, s)
            with dve.Fori(2, NT // 2) as i:
                for s in range(2):
                    step(i, 2 * i + s, s)
            step(NT // 2, NT - 1, 0)
            messages(NT - 1, 0, NT // 2, 1)
            messages(NT - 1, 0, NT // 2, 3)
            rest(NT - 1, 0, NT // 2)

            dve.wait_ge(s_zero, 1)
            accumulate(1)

            def finish(i, n, s, tiles):
                dve.wait_ge(s_rin[s], 16 * (i + 1))
                if later(i, 1):
                    dve.wait_ge(s_outst[s], 16 * i)
                dve.wait_ge(s_fint, n + 1)
                for h in range(0, tiles, 2):
                    m = min(2, tiles - h)
                    last = nc.vector.scalar_tensor_tensor(
                        out=h_out[:, s, h:h + m].rearrange("p t d -> p (t d)"),
                        in0=bank[2 * s + h // 2][:, 0:m * D], scalar=HALF,
                        in1=xin[:, s, h:h + m].rearrange("p t d -> p (t d)"), op0=ALU.mult, op1=ALU.add)
                last.then_inc(s_out, 1)

            for s in range(2):
                finish(0, s, s, ST)
            with dve.Fori(1, PAIRS) as i:
                for s in range(2):
                    finish(i, 2 * i + s, s, ST)
            finish(PAIRS, SETS, 0, 1)

        @block.tensor
        def _(pe):
            for b in range(SLOTS):
                pe.sem_inc(s_free[b], 1)
            pe.wait_ge(s_ident, 1)

            def turn_h0(n, s, tiles):
                pe.wait_ge(s_h0, n + 1)
                if later(n, 2):
                    pe.wait_ge(s_self, n - 1)
                for t in range(tiles):
                    for c in range(C):
                        last = nc.tensor.transpose(bank[2 * s + c][:, t * P:(t + 1) * P],
                                                   h_out[:, s, t, c * P:(c + 1) * P], ident[:])
                last.then_inc(s_h0t, 1)

            for s in range(2):
                turn_h0(s, s, ST)
            with pe.Fori(1, PAIRS) as i:
                for s in range(2):
                    turn_h0(2 * i + s, s, ST)
            turn_h0(SETS, 0, 1)

            n = 0
            for flat, ready in ((src_f, 1), (to_msg_f, 4), (dst_f, 5)):
                pe.wait_ge(s_float, ready)
                for b in range(NB):
                    for h in range(2):
                        if n >= 4:
                            pe.wait_ge(s_listC, n - 3)
                        for k in range(4):
                            last = nc.tensor.transpose(bank[4 + n % 4][:, k * GB:(k + 1) * GB],
                                                       flat[0:GB, b, 4 * h + k:GE:KT], ident[0:GB, 0:GB])
                        last.then_inc(s_listT, 1)
                        n += 1
            pe.wait_ge(s_listC, n)
            pe.wait_ge(s_self, SETS + 1)
            nc.tensor.matmul(bank[0][:, 0:NG], first[:], dst_all[:, :, 0], start=True, stop=True
                             ).then_inc(s_base, 1)
            pe.wait_ge(s_max, 1)
            nc.tensor.matmul(bank[1][0:1, 0:P], check[:, 0:1], ident[:], start=True, stop=True
                             ).then_inc(s_maxT, 1)
            pe.wait_ge(s_flag, 1)
            windowed = pe.value_load(in_windows[0:1, 0:1], min_val=0, max_val=1)

            def window_sums(b, q):
                for k in range(KT):
                    for c in range(C):
                        last = nc.tensor.matmul(bank[2 * q + c][:, 0:W], rows[:, b, k, c * P:(c + 1) * P],
                                                onehot[:, q, k], start=k == 0, stop=k == KT - 1)
                return last

            def accumulate(layer):
                with pe.If(windowed == 1):
                    done = layer * NG
                    with pe.Fori(0, ROUNDS) as i:
                        for b in range(SLOTS):
                            g = SLOTS * i + b
                            pe.wait_ge(s_rows[b], 16 * KT * i + 16 * KT * (layer * ROUNDS + 1))
                            pe.wait_ge(s_onehot, g + (layer * (NG + 1) + 1))
                            pe.wait_ge(s_added, g + (done + 1))
                            window_sums(b, b % 2).then_inc(s_group, 1)
                with pe.Else():
                    done = layer * NG * NT
                    with pe.Fori(0, ROUNDS) as i:
                        for b in range(SLOTS):
                            g = SLOTS * i + b
                            with pe.Fori(0, NT) as w:
                                pe.wait_ge(s_rows[b], 16 * KT * i + 16 * KT * (layer * ROUNDS + 1))
                                pe.wait_ge(s_onehot, g * NT + w + (done + 1))
                                pe.wait_ge(s_added, g * NT + w + (done + FREE_BANKS))
                                window_sums(b, 0).then_inc(s_group, 1)

            accumulate(0)
            pe.wait_ge(s_sums, 1)
            pe.wait_ge(s_weights, 16 * NCONST)

            def messages(j, s, n):
                if later(j, 1):
                    pe.wait_ge(s_msgc[n], j)
                for k in range(C):
                    last = nc.tensor.matmul(bank[n], h1t[:, s, k],
                                            wrel[:, k, RC * n:RC * (n + 1)].rearrange("p r d -> p (r d)"),
                                            start=k == 0, stop=k == C - 1)
                last.then_inc(s_msg[n], 1)

            def loop(j, s):
                if later(j, 1):
                    pe.wait_ge(s_rest, j)
                for k in range(C):
                    last = nc.tensor.matmul(bank[7][:, 0:D], h1t[:, s, k], wloop[:, k],
                                            start=k == 0, stop=k == C - 1)
                last.then_inc(s_loop, 1)

            def back(j, s):
                for n in (2, 3):
                    messages(j, s, n)
                loop(j, s)

            def step(j, s, at):
                if later(j, 1):
                    pe.wait_ge(s_hid, j)
                for o in range(C):
                    for k in range(C):
                        last = nc.tensor.matmul(bank[4][:, o * P:(o + 1) * P], w1[:, k, o * P:(o + 1) * P],
                                                sums[:, k, bass.ds(at, P)], start=k == 0, stop=k == C - 1)
                last.then_inc(s_y1, 1)
                if later(j, 1):
                    pe.wait_ge(s_h1t, j)
                    for n in (0, 1):
                        messages(j - 1, 1 - s, n)
                pe.wait_ge(s_hid, j + 1)
                if later(j, 1):
                    pe.wait_ge(s_x1, j)
                for k in range(C):
                    last = nc.tensor.matmul(bank[5][:, 0:D], hidden[:, s, k], w2[:, k],
                                            start=k == 0, stop=k == C - 1)
                last.then_inc(s_y2, 1)
                if later(j, 1):
                    back(j - 1, 1 - s)
                pe.wait_ge(s_h1, j + 1)
                for c in range(C):
                    last = nc.tensor.transpose(bank[6][:, c * P:(c + 1) * P], h_out[:, s, 0, c * P:(c + 1) * P],
                                               ident[:])
                last.then_inc(s_h1tp, 1)

            for j in range(4):
                step(j, j % 2, j * P)
            with pe.Fori(2, NT // 2) as i:
                for s in range(2):
                    step(2 * i + s, s, (2 * i + s) * P)
            step(NT - 1, 0, LAST)
            pe.wait_ge(s_h1t, NT)
            for n in (0, 1):
                messages(NT - 1, 0, n)
            back(NT - 1, 0)

            for n in range(NCH):
                pe.wait_ge(s_msgc[n], NT)
            accumulate(1)

            def turn_sums(n, s, tiles):
                pe.wait_ge(s_fin, n + 1)
                if later(n, 2):
                    pe.wait_ge(s_out, n - 1)
                for t in range(tiles):
                    for c in range(C):
                        last = nc.tensor.transpose(bank[2 * s + t // 2][:, (t % 2 * C + c) * P:][:, 0:P],
                                                   final[:, s, c, t * P:(t + 1) * P], ident[:])
                last.then_inc(s_fint, 1)

            for s in range(2):
                turn_sums(s, s, ST)
            with pe.Fori(1, PAIRS) as i:
                for s in range(2):
                    turn_sums(2 * i + s, s, ST)
            turn_sums(SETS, 0, 1)


_INS = ['x', 'src', 'dst', 'edge_type_8', 'L0_gnn_W1', 'L0_gnn_b1', 'L0_gnn_W2', 'L0_gnn_b2', 'L0_gnn_eps',
        'L1_gnn_weight', 'L1_gnn_h_bias', 'L1_gnn_loop_weight']


def kernel(**inputs):
    import numpy as _np
    import concourse.bacc as _bacc
    from concourse import mybir as _mybir
    from concourse.bass_utils import run_bass_kernel_spmd as _run

    nc = _bacc.Bacc("TRN2", target_bir_lowering=False, num_devices=1)
    arrays, args = {}, []
    for name in _INS:
        a = _np.ascontiguousarray(inputs[name])
        arrays[f"in_{name}_dram"] = a
        args.append(nc.dram_tensor(f"in_{name}_dram", a.shape, _mybir.dt.from_np(a.dtype), kind="ExternalInput").ap())
    out = nc.dram_tensor("out_dram", inputs['x'].shape, _mybir.dt.float32, kind="ExternalOutput").ap()
    gnn_program(nc, *args, out)
    r = _run(nc, [arrays], core_ids=[0])
    return r.results[0]["out_dram"]
```

```python
import concourse.bass as bass
from concourse import mybir
from contextlib import ExitStack

F32 = mybir.dt.float32
I32 = mybir.dt.int32
ALU = mybir.AluOpType
ACT = mybir.ActivationFunctionType
AX = mybir.AxisListType


def later(n, least):
    return not isinstance(n, int) or n >= least


def gnn_program(nc, x, src, dst, edge_type, W1, b1, W2, b2, eps, Wrel, rel_bias, Wloop, out):
    N, D = x.shape
    E, = src.shape
    R = Wrel.shape[0]
    P = 128
    C = D // P
    KT = 8
    GE = KT * P
    NG = -(-E // GE)
    TAIL = E - (NG - 1) * GE
    TAIL_P = TAIL // KT
    NB = 2
    GB = NG // NB
    SLOTS = 4
    ROUNDS = NG // SLOTS
    W = P
    NT = -(-N // P)
    LAST = (NT - 1) * P
    LEFT = N - LAST
    SPLIT = LEFT // 16 * 16
    EARLY = NT - 3
    ACC = N + W
    ST = 4
    SETS = (NT - 1) // ST
    PAIRS = SETS // 2
    FREE_BANKS = 2
    NCONST = 9
    PLAN = 6
    MSG_BANK = (5, 6, 7, 5)
    NOWHERE = 1 << 14
    HALF = 0.5 ** 0.5
    LN_EPS = 1e-5
    NCH = R * D // 512
    RC = 512 // D
    assert NG == NB * GB and NG == SLOTS * ROUNDS and TAIL % KT == 0 and (NT - 1) % (2 * ST) == 0
    assert NOWHERE > N + W and NCH == 4 and C == 2

    h0_rows = nc.dram_tensor("h0_rows", (N, D), F32, kind="Internal").ap()
    msg_rows = nc.dram_tensor("msg_rows", (N, R * D), F32, kind="Internal").ap()
    msg_table = msg_rows.rearrange("n (r d) -> (n r) d", r=R)
    rest_rows = nc.dram_tensor("rest_rows", (N, D), F32, kind="Internal").ap()

    with ExitStack() as ctx:
        def sb(name, shape, dt=F32):
            return ctx.enter_context(nc.sbuf_tensor(name, shape, dt))

        def sem(name):
            return ctx.enter_context(nc.semaphore(name))

        sums = sb("sums", [P, C, ACC])
        rows = sb("rows", [P, SLOTS, KT, D])
        onehot = sb("onehot", [P, 2, KT, W])
        idx_all = sb("idx_all", [P, 2, NG, KT], I32)
        idx = sb("idx", [P, SLOTS, KT], I32)
        ready = sb("ready", [1, NG])
        ready_i = sb("ready_i", [1, NG], I32)
        done_f = sb("done_f", [1, NG + 1])
        tile_i = sb("tile_i", [1, NG + 1], I32)
        turn_i = sb("turn_i", [1, NG], I32)
        ones = sb("ones", [1, NG])
        steps_back = sb("steps_back", [P, NG])
        zeros = sb("zeros", [P, C, P])
        dst_all = sb("dst_all", [P, NG, KT])
        local = sb("local", [P, NG + 1, KT])
        base_f = sb("base_f", [P, NG])
        base_i = sb("base_i", [P, NG], I32)
        check = sb("check", [P, 4])
        in_windows = sb("in_windows", [P, 1], I32)
        iota_i = sb("iota_i", [P, W], I32)
        iota_w = sb("iota_w", [P, W])
        window = sb("window", [P, W])
        part_i = sb("part_i", [P, 1], I32)
        part_f = sb("part_f", [P, 1])
        ident = sb("ident", [P, P])
        first = sb("first", [P, P])
        w1 = sb("w1", [P, C, D])
        w2 = sb("w2", [P, C, D])
        wrel = sb("wrel", [P, C, R, D])
        wloop = sb("wloop", [P, C, D])
        b1_c = sb("b1_c", [P, C])
        b2_r = sb("b2_r", [P, D])
        bias_r = sb("bias_r", [P, D])
        eps1 = sb("eps1", [P, 1])
        lneps = sb("lneps", [P, 1])
        xin = sb("xin", [P, 2, ST, D])
        h_out = sb("h_out", [P, 2, ST, D])
        stats = sb("stats", [P, 2, ST, 6])
        meanvar = sb("meanvar", [P, 2, ST, 2])
        std = sb("std", [P, 2, ST])
        rstd = sb("rstd", [P, 2, ST])
        shift = sb("shift", [P, 2, ST])
        hidden = sb("hidden", [P, C, P])
        x1 = sb("x1", [P, D])
        h1t = sb("h1t", [P, C, P])
        msg = sb("msg", [P, R * D])
        turned = sb("turned", [P, C, P])
        x_in = sb("x_in", [P, D])
        x_b2 = sb("x_b2", [P, D])
        x1_bias = sb("x1_bias", [P, D])
        rest = sb("rest", [P, D])
        h1 = sb("h1", [P, D])
        out_sb = sb("out_sb", [P, D])
        room = [rows[:, n].rearrange("p k (b f) -> p (k b f)", b=1) for n in range(SLOTS)]

        def as_blocks(ap):
            return ap.rearrange("p (b e) -> p b e", b=NB)

        src_raw, type_raw, dst_raw = (as_blocks(room[n].bitcast(I32)) for n in (0, 1, 2))
        src_f, type_f, to_msg_f, dst_f = (as_blocks(room[n]) for n in (3, 0, 1, 0))

        psum = ctx.enter_context(nc.psum_tensor("psum", [P, 8, 512], F32))
        bank = [psum[:, n] for n in range(8)]

        s_pad = sem("s_pad")
        s_lists = sem("s_lists")
        s_float = sem("s_float")
        s_const = sem("s_const")
        s_iota = sem("s_iota")
        s_ident = sem("s_ident")
        s_weights = sem("s_weights")
        s_eps_in = sem("s_eps_in")
        s_eps = sem("s_eps")
        s_listT = sem("s_listT")
        s_listC = sem("s_listC")
        s_base = sem("s_base")
        s_base_c = sem("s_base_c")
        s_local = sem("s_local")
        s_viol = sem("s_viol")
        s_max = sem("s_max")
        s_maxT = sem("s_maxT")
        s_flag = sem("s_flag")
        s_xin = [sem(f"s_xin{n}") for n in range(2)]
        s_stats = sem("s_stats")
        s_mv = sem("s_mv")
        s_std = sem("s_std")
        s_rstd = sem("s_rstd")
        s_shift = sem("s_shift")
        s_h0 = sem("s_h0")
        s_h0t = sem("s_h0t")
        s_self = sem("s_self")
        s_h0st = [sem(f"s_h0st{n}") for n in range(2)]
        s_free = [sem(f"s_free{n}") for n in range(SLOTS)]
        s_idx = [sem(f"s_idx{n}") for n in range(SLOTS)]
        s_rows = [sem(f"s_rows{n}") for n in range(SLOTS)]
        s_onehot = sem("s_onehot")
        s_group = sem("s_group")
        s_added = sem("s_added")
        s_window = sem("s_window")
        s_sums = sem("s_sums")
        s_plan = sem("s_plan")
        s_x = sem("s_x")
        s_y1 = sem("s_y1")
        s_hid = sem("s_hid")
        s_zero = sem("s_zero")
        s_y2 = sem("s_y2")
        s_xb = sem("s_xb")
        s_x1 = sem("s_x1")
        s_x1b = sem("s_x1b")
        s_stats3 = sem("s_stats3")
        s_mv3 = sem("s_mv3")
        s_std3 = sem("s_std3")
        s_rstd3 = sem("s_rstd3")
        s_shift3 = sem("s_shift3")
        s_h1 = sem("s_h1")
        s_h1tp = sem("s_h1tp")
        s_h1t = sem("s_h1t")
        s_msg = [sem(f"s_msg{n}") for n in range(NCH)]
        s_msgc = [sem(f"s_msgc{n}") for n in range(NCH)]
        s_loop = sem("s_loop")
        s_rest = sem("s_rest")
        s_msgst = sem("s_msgst")
        s_restst = sem("s_restst")
        s_rin = sem("s_rin")
        s_fin = sem("s_fin")
        s_fint = sem("s_fint")
        s_out = sem("s_out")
        s_outst = sem("s_outst")
        s_pass = {e: sem(f"s_pass_{e}") for e in ("pool", "act", "dve")}

        set_rows = "(t p) d -> p t d"
        block = ctx.enter_context(nc.Block())

        def set_of(rows_ap, n):
            return rows_ap[bass.ds(n * ST * P, ST * P), :].rearrange(set_rows, p=P)

        @block.sync
        def _(sp):
            for n in range(2):
                sp.dma_start(xin[:, n], set_of(x, n)).then_inc(s_xin[n], 16)
            for to, of in ((eps1[:], eps.partition_broadcast(P)), (b2_r[:], b2.partition_broadcast(P)),
                           (bias_r[:], rel_bias.partition_broadcast(P)),
                           (w1[:], W1.rearrange("(k p) d -> p k d", p=P)),
                           (w2[:], W2.rearrange("(k p) d -> p k d", p=P)),
                           (wloop[:], Wloop.rearrange("(k p) d -> p k d", p=P)),
                           (wrel[:, 0], Wrel[:, 0:P].rearrange("r p d -> p r d")),
                           (wrel[:, 1], Wrel[:, P:D].rearrange("r p d -> p r d"))):
                sp.dma_start(to, of).then_inc(s_weights, 16)
            sp.dma_start(b1_c[:], b1.rearrange("(o p) -> p o", p=P), allow_slow_non_contiguous=True
                         ).then_inc(s_weights, 16)
            sp.wait_ge(s_pad, 1)
            for raw, flat in ((src_raw, src), (type_raw, edge_type), (dst_raw, dst)):
                g = 0
                for b, m in ((0, GB), (1, GB - 2), (1, 1)):
                    p0 = g - GB * b
                    sp.dma_start(raw[p0:p0 + m, b, :],
                                 flat[g * GE:(g + m) * GE].rearrange("(g e) -> g e", e=GE)).then_inc(s_lists, 16)
                    g += m
                sp.dma_start(raw[GB - 1:GB, 1, 0:TAIL],
                             flat[(NG - 1) * GE:E].rearrange("(g e) -> g e", g=1)).then_inc(s_lists, 16)

            def h0_set(i, n, s, tiles, then):
                sp.wait_ge(s_h0, n + 1)
                if tiles == ST:
                    sp.dma_start(set_of(h0_rows, n), h_out[:, s]).then_inc(s_h0st[s], 16)
                else:
                    for a, z in ((0, SPLIT), (SPLIT, LEFT)):
                        sp.dma_start(h0_rows[LAST + a:LAST + z, :], h_out[a:z, s, 0]).then_inc(s_h0st[s], 16)
                if then == ST:
                    sp.dma_start(xin[:, s], set_of(x, n + 2)).then_inc(s_xin[s], 16)
                elif then:
                    sp.dma_start(xin[0:LEFT, s, 0], x[LAST:N, :]).then_inc(s_xin[s], 16)

            with sp.Fori(0, PAIRS - 1) as i:
                for s in range(2):
                    h0_set(i, 2 * i + s, s, ST, ST)
            h0_set(PAIRS - 1, SETS - 2, 0, ST, 1)
            h0_set(PAIRS - 1, SETS - 1, 1, ST, 0)
            h0_set(PAIRS, SETS, 0, 1, 0)

            def feed(layer):
                with sp.Fori(0, ROUNDS) as i:
                    for b in range(SLOTS):
                        sp.wait_ge(s_free[b], i + (layer * ROUNDS + 1))
                        sp.dma_start(idx[:, b], idx_all[:, layer, bass.ds(SLOTS * i + b, 1), :].rearrange(
                            "p g k -> p (g k)")).then_inc(s_idx[b], 16)

            sp.wait_ge(s_listC, 4)
            feed(0)
            sp.wait_ge(s_listC, 8)
            feed(1)

        @block.gpsimd
        def _(pool):
            nc.gpsimd.iota(iota_i[:], pattern=[[1, W]], base=0, channel_multiplier=0)
            nc.gpsimd.iota(part_i[:], pattern=[[0, 1]], base=0, channel_multiplier=1).then_inc(s_const, 1)
            nc.gpsimd.memset(src_raw, 0)
            nc.gpsimd.memset(type_raw, 0)
            nc.gpsimd.memset(dst_raw, NOWHERE).then_inc(s_pad, 1)
            pool.wait_ge(s_lists, 16 * 12)
            nc.gpsimd.tensor_copy(src_f, src_raw).then_inc(s_float, 1)
            pool.wait_ge(s_float, 1)
            nc.gpsimd.tensor_copy(type_f, type_raw).then_inc(s_float, 1)
            pool.wait_ge(s_float, 2)
            nc.gpsimd.tensor_scalar(to_msg_f, src_f, float(R), None, ALU.mult).then_inc(s_float, 1)
            pool.wait_ge(s_float, 3)
            nc.gpsimd.tensor_tensor(to_msg_f, to_msg_f, type_f, ALU.add).then_inc(s_float, 1)
            pool.wait_ge(s_float, 4)
            nc.gpsimd.tensor_copy(dst_f, dst_raw).then_inc(s_float, 1)

            def gather(layer, table):
                with pool.Fori(0, ROUNDS) as i:
                    for b in range(SLOTS):
                        pool.wait_ge(s_idx[b], 16 * i + 16 * (layer * ROUNDS + 1))
                        pool.sem_inc(s_pass["pool"], 1)
                        for k in range(KT):
                            pool.indirect_dma_start(
                                out=rows[:, b, k], out_offset=None, in_=table,
                                in_offset=bass.IndirectOffsetOnAxis(ap=idx[:, b, k:k + 1], axis=0),
                            ).then_inc(s_rows[b], 16)

            pool.wait_ge(s_h0st[0], 16 * (PAIRS + 2))
            pool.wait_ge(s_h0st[1], 16 * PAIRS)
            pool.wait_ge(s_listT, 12)
            gather(0, h0_rows)
            pool.wait_ge(s_msgst, 16 * (NT + 1))
            gather(1, msg_table)

        @block.scalar
        def _(act):
            def h0_set(i, n, s, tiles):
                act.wait_ge(s_mv, n + 1)
                nc.scalar.activation(std[:, s, 0:tiles], meanvar[:, s, 0:tiles, 1], ACT.Sqrt,
                                     bias=lneps[:]).then_inc(s_std, 1)
                act.wait_ge(s_shift, n + 1)
                if later(n, 2):
                    act.wait_ge(s_h0t, n - 1)
                    act.wait_ge(s_h0st[s], 16 * i)
                for t in range(tiles):
                    last = nc.scalar.activation(h_out[:, s, t], xin[:, s, t], ACT.Relu,
                                                bias=shift[:, s, t:t + 1], scale=rstd[:, s, t:t + 1])
                last.then_inc(s_h0, 1)

            act.wait_ge(s_iota, 1)
            for s in range(2):
                h0_set(0, s, s, ST)
            with act.Fori(1, PAIRS) as i:
                for s in range(2):
                    h0_set(i, 2 * i + s, s, ST)
            h0_set(PAIRS, SETS, 0, 1)

            for n in range(3 * NB * 2):
                a, b, h = n // (NB * 2), n // 2 % NB, n % 2
                act.wait_ge(s_listT, n + 1)
                to = idx_all[:, a] if a < 2 else dst_all[:]
                nc.scalar.copy(to[:, b * GB:(b + 1) * GB, 4 * h:4 * h + 4].rearrange("p g k -> p k g"),
                               bank[4 + n % 4][:, 0:4 * GB].rearrange("p (k g) -> p k g", k=4)
                               ).then_inc(s_listC, 1)
            act.wait_ge(s_weights, 16 * NCONST)
            act.wait_ge(s_plan, PLAN)
            early = act.value_load(tile_i[0:1, NG:NG + 1], min_val=0, max_val=EARLY)
            act.dma_start(x_in[:], x[0:P, :]).then_inc(s_x, 16)

            def load(to, rows_ap, j, count):
                if isinstance(j, int) and j == NT - 1:
                    act.dma_start(to[0:LEFT], rows_ap[LAST:N, :]).then_inc(count, 16)
                elif not isinstance(j, int) or j < NT:
                    act.dma_start(to[:], rows_ap[bass.ds(j * P, P), :]).then_inc(count, 16)

            def store(rows_ap, j, of, count):
                if isinstance(j, int) and j == NT - 1:
                    for a, z in ((0, SPLIT), (SPLIT, LEFT)):
                        act.dma_start(rows_ap[LAST + a:LAST + z, :], of[a:z]).then_inc(count, 16)
                else:
                    act.dma_start(rows_ap[bass.ds(j * P, P), :], of[:]).then_inc(count, 16)

            def messages(j, n):
                act.wait_ge(s_msg[n], j + 1)
                nc.scalar.copy(msg[:, 512 * n:512 * (n + 1)], bank[MSG_BANK[n]]).then_inc(s_msgc[n], 1)

            def dense(j, g, done):
                act.wait_ge(s_y1, j + 1)
                for o in range(C):
                    last = nc.scalar.activation(hidden[:, o], bank[4][:, o * P:(o + 1) * P], ACT.Relu,
                                                bias=b1_c[:, o:o + 1])
                last.then_inc(s_hid, 1)
                nc.scalar.copy(sums[:, :, bass.ds(j * P, P)], zeros[:]).then_inc(s_zero, 1)
                act.wait_ge(s_mv3, j + 1)
                nc.scalar.activation(std[:, 0, 0:1], meanvar[:, 0, 0, 1:2], ACT.Sqrt,
                                     bias=lneps[:]).then_inc(s_std3, 1)
                act.wait_ge(s_xb, j + 1)
                load(x_in, x, j + 1, s_x)
                act.wait_ge(s_shift3, j + 1)
                nc.scalar.activation(h1[:], x1[:], ACT.Relu, bias=shift[:, 0, 0:1], scale=rstd[:, 0, 0:1]
                                     ).then_inc(s_h1, 1)
                act.wait_ge(s_h1tp, j + 1)
                nc.scalar.copy(h1t[:], bank[4][:, 0:C * P].rearrange("p (c n) -> p c n", c=C)
                               ).then_inc(s_h1t, 1)
                act.wait_ge(s_msgst, 16 * j)
                messages(j, 0)
                messages(j, 2)
                for n in range(NCH):
                    act.wait_ge(s_msgc[n], j + 1)
                store(msg_rows, j, msg, s_msgst)
                act.wait_ge(s_rest, j + 1)
                store(rest_rows, j, rest, s_restst)

            def finish(j, g, done):
                if g is not None:
                    act.wait_ge(s_added, g + (done + FREE_BANKS))
                act.sem_inc(s_pass["act"], 1)
                nc.scalar.copy(turned[:], sums[:, :, bass.ds(j * P, P)]).then_inc(s_fin, 1)
                act.wait_ge(s_out, j + 1)
                store(out, j, out_sb, s_outst)
                load(rest, rest_rows, j + 1, s_rin)

            def tiles(layer, work):
                with act.Fori(0, ROUNDS) as i:
                    for b in range(SLOTS):
                        g = SLOTS * i + b
                        turn = act.value_load(turn_i[0:1, bass.ds(g, 1)], min_val=0, max_val=1)
                        with act.If(turn == 1):
                            j = act.value_load(tile_i[0:1, bass.ds(g, 1)], min_val=0, max_val=EARLY)
                            work(j, g, layer * NG)
                act.wait_ge(s_sums, layer + 1)
                with act.Fori(early, NT - 2) as j:
                    work(j, None, 0)
                for j in (NT - 2, NT - 1):
                    work(j, None, 0)

            tiles(0, dense)
            act.wait_ge(s_restst, 16 * (NT + 1))
            load(rest, rest_rows, 0, s_rin)
            tiles(1, finish)
            act.wait_ge(s_outst, 16 * (NT + 1))

        @block.vector
        def _(dve):
            def stage_in(i, n, s, tiles):
                dve.wait_ge(s_xin[s], 16 * (i + 1))
                for t in range(tiles):
                    last = nc.vector.bn_stats(stats[:, s, t], xin[:, s, t])
                last.then_inc(s_stats, 1)
                dve.wait_ge(s_stats, n + 1)
                dve.sem_inc(s_pass["dve"], 1)
                for t in range(tiles):
                    last = nc.vector.bn_aggr(meanvar[:, s, t], stats[:, s, t])
                last.then_inc(s_mv, 1)

            def stage_norm(n, s, tiles):
                dve.wait_ge(s_std, n + 1)
                nc.vector.reciprocal(rstd[:, s, 0:tiles], std[:, s, 0:tiles]).then_inc(s_rstd, 1)
                dve.wait_ge(s_rstd, n + 1)
                nc.vector.scalar_tensor_tensor(out=shift[:, s, 0:tiles], in0=meanvar[:, s, 0:tiles, 0],
                                               scalar=-1.0, in1=rstd[:, s, 0:tiles],
                                               op0=ALU.mult, op1=ALU.mult).then_inc(s_shift, 1)

            def stage_self(n, s, tiles):
                at = n * (ST * P) if tiles == ST else LAST
                dve.wait_ge(s_h0t, n + 1)
                for c in range(C):
                    last = nc.vector.tensor_scalar(sums[:, c, bass.ds(at, tiles * P)],
                                                   bank[2 * s + c][:, 0:tiles * P], eps1[:], None, ALU.mult)
                last.then_inc(s_self, 1)

            nc.vector.memset(lneps[:], LN_EPS)
            nc.vector.memset(first[:], 0.0)
            nc.vector.memset(zeros[:], 0.0)
            nc.vector.memset(ones[:], 1.0)
            nc.vector.memset(done_f[:], 0.0)
            nc.vector.memset(local[:, NG], -1.0)
            nc.vector.memset(sums[:, :, N:ACC], 0.0).then_inc(s_iota, 1)
            dve.wait_ge(s_const, 1)
            nc.vector.tensor_copy(iota_w[:], iota_i[:])
            nc.vector.tensor_copy(part_f[:], part_i[:]).then_inc(s_iota, 1)
            dve.wait_ge(s_iota, 2)
            nc.vector.memset(first[0:1, :], 1.0)
            nc.vector.tensor_scalar(ident[:], iota_w[:], part_f[:], None, ALU.is_equal).then_inc(s_ident, 1)
            dve.wait_ge(s_weights, 16 * NCONST)
            nc.vector.tensor_scalar_add(eps1[:], eps1[:], 1.0).then_inc(s_eps, 1)
            dve.wait_ge(s_eps, 1)

            stage_in(0, 0, 0, ST)
            stage_norm(0, 0, ST)
            stage_in(0, 1, 1, ST)
            stage_self(0, 0, ST)
            stage_norm(1, 1, ST)
            with dve.Fori(1, PAIRS) as i:
                for s in range(2):
                    stage_in(i, 2 * i + s, s, ST)
                    stage_self(2 * i + s - 1, 1 - s, ST)
                    stage_norm(2 * i + s, s, ST)
            stage_in(PAIRS, SETS, 0, 1)
            stage_self(SETS - 1, 1, ST)
            stage_norm(SETS, 0, 1)
            stage_self(SETS, 0, 1)

            dve.wait_ge(s_base, 1)
            nc.vector.tensor_copy(base_f[:], bank[0][:, 0:NG])
            nc.vector.tensor_copy(base_i[:], bank[0][:, 0:NG]).then_inc(s_base_c, 1)
            dve.wait_ge(s_base_c, 1)
            nc.vector.tensor_tensor(local[:, 0:NG], dst_all[:], base_f[:].unsqueeze(2).broadcast_to([P, NG, KT]),
                                    ALU.subtract).then_inc(s_local, 1)
            dve.wait_ge(s_local, 1)
            mid = onehot[:, 0:2].rearrange("p q k w -> p (q k w)")[:, 0:NG * KT].rearrange("p (g k) -> p g k", k=KT)
            nc.vector.tensor_scalar(mid, local[:, 0:NG], -(W - 1) / 2, None, ALU.add).then_inc(s_viol, 1)
            dve.wait_ge(s_viol, 1)
            nc.vector.tensor_reduce(check[:, 0:1], mid[:, 0:NG - 1], axis=AX.XY, op=ALU.max,
                                    apply_absolute_value=True)
            nc.vector.tensor_reduce(check[0:TAIL_P, 2:3], mid[0:TAIL_P, NG - 1], axis=AX.X, op=ALU.max,
                                    apply_absolute_value=True).then_inc(s_viol, 1)
            dve.wait_ge(s_viol, 2)
            nc.vector.tensor_tensor(check[0:TAIL_P, 0:1], check[0:TAIL_P, 0:1], check[0:TAIL_P, 2:3],
                                    ALU.max).then_inc(s_viol, 1)
            nc.vector.tensor_tensor(steps_back[:, 0:NG - 1], base_f[:, 0:NG - 1], base_f[:, 1:NG],
                                    ALU.subtract).then_inc(s_viol, 1)
            dve.wait_ge(s_viol, 4)
            nc.vector.tensor_reduce(check[:, 3:4], steps_back[:, 0:NG - 1], axis=AX.X, op=ALU.max
                                    ).then_inc(s_viol, 1)
            dve.wait_ge(s_viol, 5)
            nc.vector.scalar_tensor_tensor(out=check[:, 0:1], in0=check[:, 3:4], scalar=float(W),
                                           in1=check[:, 0:1], op0=ALU.mult, op1=ALU.max).then_inc(s_max, 1)
            dve.wait_ge(s_maxT, 1)
            nc.vector.tensor_reduce(check[0:1, 1:2], bank[1][0:1, 0:P], axis=AX.X, op=ALU.max).then_inc(s_max, 1)
            dve.wait_ge(s_max, 2)
            nc.vector.tensor_scalar(in_windows[0:1, :], check[0:1, 1:2], W / 2, None, ALU.is_lt).then_inc(s_flag, 1)
            nc.vector.tensor_scalar(ready_i[:], base_i[0:1, :], W.bit_length() - 1, None, ALU.arith_shift_right
                                    ).then_inc(s_plan, 1)
            dve.wait_ge(s_plan, 1)
            nc.vector.tensor_scalar(ready[:], ready_i[:], float(EARLY), None, ALU.min).then_inc(s_plan, 1)
            dve.wait_ge(s_plan, 2)
            dve.wait_ge(s_flag, 1)
            nc.vector.tensor_copy(check[0:1, 2:3], in_windows[0:1, :]).then_inc(s_plan, 1)
            dve.wait_ge(s_plan, 3)
            nc.vector.tensor_scalar(ready[:], ready[:], check[0:1, 2:3], None, ALU.mult).then_inc(s_plan, 1)
            dve.wait_ge(s_plan, 4)
            nc.vector.tensor_tensor_scan(out=done_f[:, 1:NG + 1], data0=ones[:], data1=ready[:], initial=0.0,
                                         op0=ALU.add, op1=ALU.min).then_inc(s_plan, 1)
            dve.wait_ge(s_plan, 5)
            nc.vector.tensor_copy(tile_i[:], done_f[:])
            nc.vector.tensor_tensor(turn_i[:], done_f[:, 1:NG + 1], done_f[:, 0:NG], ALU.subtract
                                    ).then_inc(s_plan, 1)
            dve.wait_ge(s_plan, PLAN)
            windowed = dve.value_load(in_windows[0:1, 0:1], min_val=0, max_val=1)

            def one_hots(q, nodes, dests):
                return nc.vector.tensor_tensor(
                    onehot[:, q], nodes.unsqueeze(1).broadcast_to([P, KT, W]),
                    dests.rearrange("p g k -> p (g k)").unsqueeze(2).broadcast_to([P, KT, W]), ALU.is_equal)

            def add(q, at):
                cols = sums[:, :, bass.ds(at, W)]
                return nc.vector.tensor_tensor(cols, cols, psum[:, 2 * q:2 * q + C, 0:W], ALU.add)

            early = dve.value_load(tile_i[0:1, NG:NG + 1], min_val=0, max_val=EARLY)

            def accumulate(layer, before, after):
                with dve.If(windowed == 1):
                    done = layer * NG
                    one_hots(0, iota_w[:], local[:, 0:1, :]).then_inc(s_onehot, 1)
                    with dve.Fori(0, ROUNDS) as i:
                        for b in range(SLOTS):
                            g, q = SLOTS * i + b, b % 2
                            at = dve.value_load(base_i[0:1, bass.ds(g, 1)], min_val=0, max_val=N - 1)
                            turn = dve.value_load(turn_i[0:1, bass.ds(g, 1)], min_val=0, max_val=1)
                            j = dve.value_load(tile_i[0:1, bass.ds(g, 1)], min_val=0, max_val=EARLY)
                            one_hots(1 - q, iota_w[:], local[:, bass.ds(g + 1, 1), :]).then_inc(s_onehot, 1)
                            with dve.If(turn == 1):
                                before(j)
                            dve.wait_ge(s_group, g + (done + 1))
                            dve.sem_inc(s_free[b], 1)
                            dve.wait_ge(s_added, g + (done + FREE_BANKS))
                            add(q, at).then_inc(s_added, 1)
                            with dve.If(turn == 1):
                                after(j)
                    dve.wait_ge(s_added, done + NG + FREE_BANKS)
                with dve.Else():
                    done = layer * NG * NT
                    with dve.Fori(0, ROUNDS) as i:
                        for b in range(SLOTS):
                            g = SLOTS * i + b
                            nc.vector.tensor_scalar(window[:], iota_w[:], -float(W), None, ALU.add
                                                    ).then_inc(s_window, 1)
                            with dve.Fori(0, NT) as w:
                                n = g * NT + w
                                dve.wait_ge(s_window, n + g + (layer * NG * (NT + 1) + 1))
                                nc.vector.tensor_scalar(window[:], window[:], float(W), None, ALU.add
                                                        ).then_inc(s_window, 1)
                                dve.wait_ge(s_window, n + g + (layer * NG * (NT + 1) + 2))
                                one_hots(0, window[:], dst_all[:, bass.ds(g, 1), :]).then_inc(s_onehot, 1)
                                dve.wait_ge(s_group, n + (done + 1))
                                dve.wait_ge(s_added, n + (done + FREE_BANKS))
                                add(0, w * W).then_inc(s_added, 1)
                            dve.sem_inc(s_free[b], 1)
                    dve.wait_ge(s_added, done + NG * NT + FREE_BANKS)
                dve.sem_inc(s_sums, 1)
                with dve.Fori(early, NT) as j:
                    before(j)
                    after(j)

            dve.wait_ge(s_self, SETS + 1)
            dve.sem_inc(s_added, FREE_BANKS)

            def dense_before(j):
                dve.wait_ge(s_x, 16 * j + 16)
                nc.vector.tensor_tensor(x_b2[:], x_in[:], b2_r[:], ALU.add).then_inc(s_xb, 1)
                dve.wait_ge(s_xb, j + 1)
                dve.wait_ge(s_y2, j + 1)
                nc.vector.tensor_tensor(x1[:], x_b2[:], bank[4][:, C * P:C * P + D], ALU.add).then_inc(s_x1, 1)
                dve.wait_ge(s_x1, j + 1)
                nc.vector.bn_stats(stats[:, 0, 0], x1[:]).then_inc(s_stats3, 1)
                dve.wait_ge(s_stats3, j + 1)
                dve.sem_inc(s_pass["dve"], 1)
                nc.vector.bn_aggr(meanvar[:, 0, 0], stats[:, 0, 0]).then_inc(s_mv3, 1)
                dve.wait_ge(s_std3, j + 1)
                nc.vector.reciprocal(rstd[:, 0, 0:1], std[:, 0, 0:1]).then_inc(s_rstd3, 1)
                dve.wait_ge(s_rstd3, j + 1)
                nc.vector.scalar_tensor_tensor(out=shift[:, 0, 0:1], in0=meanvar[:, 0, 0, 0:1], scalar=-1.0,
                                               in1=rstd[:, 0, 0:1], op0=ALU.mult, op1=ALU.mult
                                               ).then_inc(s_shift3, 1)
                nc.vector.tensor_tensor(x1_bias[:], x1[:], bias_r[:], ALU.add).then_inc(s_x1b, 1)

            def messages(j, n):
                dve.wait_ge(s_msg[n], j + 1)
                nc.vector.tensor_copy(msg[:, 512 * n:512 * (n + 1)], bank[MSG_BANK[n]]).then_inc(s_msgc[n], 1)

            def dense_after(j):
                dve.wait_ge(s_msgst, 16 * j)
                messages(j, 1)
                dve.wait_ge(s_x1b, j + 1)
                dve.wait_ge(s_restst, 16 * j)
                dve.wait_ge(s_loop, j + 1)
                nc.vector.scalar_tensor_tensor(out=rest[:], in0=bank[4][:, C * P:C * P + D], scalar=HALF,
                                               in1=x1_bias[:], op0=ALU.mult, op1=ALU.add).then_inc(s_rest, 1)
                messages(j, 3)

            accumulate(0, dense_before, dense_after)

            def finish(j):
                dve.wait_ge(s_rin, 16 * j + 16)
                dve.wait_ge(s_outst, 16 * j)
                dve.wait_ge(s_fint, j + 1)
                nc.vector.scalar_tensor_tensor(out=out_sb[:], in0=bank[5][:, 0:D], scalar=HALF,
                                               in1=rest[:], op0=ALU.mult, op1=ALU.add).then_inc(s_out, 1)

            dve.wait_ge(s_zero, NT)
            accumulate(1, lambda j: None, finish)

        @block.tensor
        def _(pe):
            for b in range(SLOTS):
                pe.sem_inc(s_free[b], 1)
            pe.wait_ge(s_ident, 1)

            def turn_h0(n, s, tiles):
                pe.wait_ge(s_h0, n + 1)
                if later(n, 2):
                    pe.wait_ge(s_self, n - 1)
                for t in range(tiles):
                    for c in range(C):
                        last = nc.tensor.transpose(bank[2 * s + c][:, t * P:(t + 1) * P],
                                                   h_out[:, s, t, c * P:(c + 1) * P], ident[:])
                last.then_inc(s_h0t, 1)

            for s in range(2):
                turn_h0(s, s, ST)
            with pe.Fori(1, PAIRS) as i:
                for s in range(2):
                    turn_h0(2 * i + s, s, ST)
            turn_h0(SETS, 0, 1)

            n = 0
            for flat, ready in ((src_f, 1), (to_msg_f, 4), (dst_f, 5)):
                pe.wait_ge(s_float, ready)
                for b in range(NB):
                    for h in range(2):
                        if n >= 4:
                            pe.wait_ge(s_listC, n - 3)
                        for k in range(4):
                            last = nc.tensor.transpose(bank[4 + n % 4][:, k * GB:(k + 1) * GB],
                                                       flat[0:GB, b, 4 * h + k:GE:KT], ident[0:GB, 0:GB])
                        last.then_inc(s_listT, 1)
                        n += 1
            pe.wait_ge(s_listC, n)
            pe.wait_ge(s_self, SETS + 1)
            nc.tensor.matmul(bank[0][:, 0:NG], first[:], dst_all[:, :, 0], start=True, stop=True
                             ).then_inc(s_base, 1)
            pe.wait_ge(s_max, 1)
            nc.tensor.matmul(bank[1][0:1, 0:P], check[:, 0:1], ident[:], start=True, stop=True
                             ).then_inc(s_maxT, 1)
            pe.wait_ge(s_plan, PLAN)
            windowed = pe.value_load(in_windows[0:1, 0:1], min_val=0, max_val=1)

            def window_sums(b, q):
                for k in range(KT):
                    for c in range(C):
                        last = nc.tensor.matmul(bank[2 * q + c][:, 0:W], rows[:, b, k, c * P:(c + 1) * P],
                                                onehot[:, q, k], start=k == 0, stop=k == KT - 1)
                return last

            early = pe.value_load(tile_i[0:1, NG:NG + 1], min_val=0, max_val=EARLY)

            def accumulate(layer, before, after):
                with pe.If(windowed == 1):
                    done = layer * NG
                    with pe.Fori(0, ROUNDS) as i:
                        for b in range(SLOTS):
                            g = SLOTS * i + b
                            turn = pe.value_load(turn_i[0:1, bass.ds(g, 1)], min_val=0, max_val=1)
                            j = pe.value_load(tile_i[0:1, bass.ds(g, 1)], min_val=0, max_val=EARLY)
                            with pe.If(turn == 1):
                                pe.wait_ge(s_added, g + (done + FREE_BANKS))
                                before(j)
                            pe.wait_ge(s_rows[b], 16 * KT * i + 16 * KT * (layer * ROUNDS + 1))
                            pe.wait_ge(s_onehot, g + (layer * (NG + 1) + 1))
                            pe.wait_ge(s_added, g + (done + 1))
                            window_sums(b, b % 2).then_inc(s_group, 1)
                            with pe.If(turn == 1):
                                after(j)
                with pe.Else():
                    done = layer * NG * NT
                    with pe.Fori(0, ROUNDS) as i:
                        for b in range(SLOTS):
                            g = SLOTS * i + b
                            with pe.Fori(0, NT) as w:
                                pe.wait_ge(s_rows[b], 16 * KT * i + 16 * KT * (layer * ROUNDS + 1))
                                pe.wait_ge(s_onehot, g * NT + w + (done + 1))
                                pe.wait_ge(s_added, g * NT + w + (done + FREE_BANKS))
                                window_sums(b, 0).then_inc(s_group, 1)
                pe.wait_ge(s_sums, layer + 1)
                with pe.Fori(early, NT) as j:
                    before(j)
                    after(j)

            pe.wait_ge(s_weights, 16 * NCONST)

            def dense_before(j):
                pe.wait_ge(s_rest, j)
                for o in range(C):
                    for k in range(C):
                        last = nc.tensor.matmul(bank[4][:, o * P:(o + 1) * P], w1[:, k, o * P:(o + 1) * P],
                                                sums[:, k, bass.ds(j * P, P)], start=k == 0, stop=k == C - 1)
                last.then_inc(s_y1, 1)
                pe.wait_ge(s_hid, j + 1)
                for k in range(C):
                    last = nc.tensor.matmul(bank[4][:, C * P:C * P + D], hidden[:, k], w2[:, k],
                                            start=k == 0, stop=k == C - 1)
                last.then_inc(s_y2, 1)

            def messages(j, n):
                for k in range(C):
                    last = nc.tensor.matmul(bank[MSG_BANK[n]], h1t[:, k],
                                            wrel[:, k, RC * n:RC * (n + 1)].rearrange("p r d -> p (r d)"),
                                            start=k == 0, stop=k == C - 1)
                last.then_inc(s_msg[n], 1)

            def dense_after(j):
                pe.wait_ge(s_h1, j + 1)
                for c in range(C):
                    last = nc.tensor.transpose(bank[4][:, c * P:(c + 1) * P], h1[:, c * P:(c + 1) * P], ident[:])
                last.then_inc(s_h1tp, 1)
                pe.wait_ge(s_h1t, j + 1)
                for n, before in ((0, 3), (1, 1), (2, 2)):
                    pe.wait_ge(s_msgc[before], j)
                    messages(j, n)
                for k in range(C):
                    last = nc.tensor.matmul(bank[4][:, C * P:C * P + D], h1t[:, k], wloop[:, k],
                                            start=k == 0, stop=k == C - 1)
                last.then_inc(s_loop, 1)
                pe.wait_ge(s_msgc[0], j + 1)
                messages(j, 3)

            accumulate(0, dense_before, dense_after)

            def finish(j):
                pe.wait_ge(s_fin, j + 1)
                pe.wait_ge(s_out, j)
                for c in range(C):
                    last = nc.tensor.transpose(bank[5][:, c * P:(c + 1) * P], turned[:, c], ident[:])
                last.then_inc(s_fint, 1)

            pe.wait_ge(s_msgc[3], NT)
            accumulate(1, lambda j: None, finish)


_INS = ['x', 'src', 'dst', 'edge_type_8', 'L0_gnn_W1', 'L0_gnn_b1', 'L0_gnn_W2', 'L0_gnn_b2', 'L0_gnn_eps',
        'L1_gnn_weight', 'L1_gnn_h_bias', 'L1_gnn_loop_weight']


def kernel(**inputs):
    import numpy as _np
    import concourse.bacc as _bacc
    from concourse import mybir as _mybir
    from concourse.bass_utils import run_bass_kernel_spmd as _run

    nc = _bacc.Bacc("TRN2", target_bir_lowering=False, num_devices=1)
    arrays, args = {}, []
    for name in _INS:
        a = _np.ascontiguousarray(inputs[name])
        arrays[f"in_{name}_dram"] = a
        args.append(nc.dram_tensor(f"in_{name}_dram", a.shape, _mybir.dt.from_np(a.dtype), kind="ExternalInput").ap())
    out = nc.dram_tensor("out_dram", inputs['x'].shape, _mybir.dt.float32, kind="ExternalOutput").ap()
    gnn_program(nc, *args, out)
    r = _run(nc, [arrays], core_ids=[0])
    return r.results[0]["out_dram"]
```

```python
import concourse.bass as bass
from concourse import mybir
from contextlib import ExitStack

F32 = mybir.dt.float32
I32 = mybir.dt.int32
ALU = mybir.AluOpType
ACT = mybir.ActivationFunctionType
AX = mybir.AxisListType


def later(n, least):
    return not isinstance(n, int) or n >= least


def gnn_program(nc, x, src, dst, edge_type, W1, b1, W2, b2, eps, Wrel, rel_bias, Wloop, out):
    N, D = x.shape
    E, = src.shape
    R = Wrel.shape[0]
    P = 128
    C = D // P
    KT = 8
    GE = KT * P
    NG = -(-E // GE)
    TAIL = E - (NG - 1) * GE
    WHOLE, OVER = divmod(TAIL, P)
    LIST_BANKS = 4
    PADDED = KT - WHOLE - 1
    NB = 2
    GB = NG // NB
    SLOTS = 4
    ROUNDS = NG // SLOTS
    W = 80
    NW = -(-N // W)
    NT = -(-N // P)
    LAST = (NT - 1) * P
    LEFT = N - LAST
    SPLIT = LEFT // 16 * 16
    EARLY = NT - 1
    ACC = N + W
    ST = 4
    SETS = (NT - 1) // ST
    XS = 4
    TURNS = SETS // XS
    FREE_BANKS = 2
    NCONST = 8
    PLAN = 6
    MSG_BANK = (4, 5, 6, 7)
    PAD_P = (GB - 1) // 32 * 32
    AHEAD = 2
    NOWHERE = 1 << 14
    HALF = 0.5 ** 0.5
    LN_EPS = 1e-5
    NCH = R * D // 512
    RC = 512 // D
    assert NG == NB * GB and NG == SLOTS * ROUNDS and NB * 2 == LIST_BANKS and 0 < OVER < P and OVER % 32 == 0
    assert (NT - 1) % (XS * ST) == 0
    assert NOWHERE > N + W and NCH == 4 and C == 2

    h0_rows = nc.dram_tensor("h0_rows", (N, D), F32, kind="Internal").ap()
    msg_rows = nc.dram_tensor("msg_rows", (NT * P, R * D), F32, kind="Internal").ap()
    msg_table = msg_rows.rearrange("n (r d) -> (n r) d", r=R)
    rest_rows = nc.dram_tensor("rest_rows", (NT * P, D), F32, kind="Internal").ap()

    with ExitStack() as ctx:
        def sb(name, shape, dt=F32):
            return ctx.enter_context(nc.sbuf_tensor(name, shape, dt))

        def sem(name):
            return ctx.enter_context(nc.semaphore(name))

        sums = sb("sums", [P, C, ACC])
        rows = sb("rows", [P, SLOTS, KT, D])
        onehot = sb("onehot", [P, 2, KT, P])
        idx_all = sb("idx_all", [P, 2, NG, KT], I32)
        idx = sb("idx", [P, SLOTS, KT], I32)
        ready = sb("ready", [1, NG])
        ready_i = sb("ready_i", [1, NG], I32)
        done_f = sb("done_f", [1, NG + 2])
        tile_i = sb("tile_i", [1, NG + 2], I32)
        ones = sb("ones", [1, NG])
        steps_back = sb("steps_back", [P, NG])
        zeros = sb("zeros", [P, C, P])
        dst_all = sb("dst_all", [P, NG, KT])
        local = sb("local", [P, NG, KT])
        base_f = sb("base_f", [P, NG])
        base_i = sb("base_i", [P, NG], I32)
        check = sb("check", [P, 4])
        in_windows = sb("in_windows", [P, 1], I32)
        iota_i = sb("iota_i", [P, P], I32)
        iota_p = sb("iota_p", [P, P])
        window = sb("window", [P, W])
        part_i = sb("part_i", [P, 1], I32)
        part_f = sb("part_f", [P, 1])
        ident = sb("ident", [P, P])
        first = sb("first", [P, P])
        w1 = sb("w1", [P, C, D])
        w2 = sb("w2", [P, C, D])
        wrel = sb("wrel", [P, C, R, D])
        wloop = sb("wloop", [P, C, D])
        b1_c = sb("b1_c", [P, C])
        b2_r = sb("b2_r", [P, D])
        bias_r = sb("bias_r", [P, D])
        eps1 = sb("eps1", [P, 1])
        lneps = sb("lneps", [P, 1])
        xin = sb("xin", [P, XS, ST, D])
        h_out = sb("h_out", [P, 2, ST, D])
        stats = sb("stats", [P, 2, ST, 6])
        meanvar = sb("meanvar", [P, 2, ST, 2])
        std = sb("std", [P, 2, ST])
        rstd = sb("rstd", [P, 2, ST])
        shift = sb("shift", [P, 2, ST])
        hidden = sb("hidden", [P, C, P])
        x1 = sb("x1", [P, D])
        h1t = sb("h1t", [P, C, P])
        msg = sb("msg", [P, R * D])
        turned = sb("turned", [P, C, P])
        x_in = sb("x_in", [P, D])
        x_b2 = sb("x_b2", [P, D])
        x1_bias = sb("x1_bias", [P, D])
        rest = sb("rest", [P, D])
        h1 = sb("h1", [P, D])
        out_sb = sb("out_sb", [P, D])
        room = [wrel[:, 0], wrel[:, 1], msg[:].rearrange("p (r d) -> p r d", r=R),
                onehot[:].rearrange("p q k w -> p (q k w)").rearrange("p (r d) -> p r d", r=R)]

        def as_blocks(ap):
            return ap[0:GB].rearrange("p r d -> p (r d)").rearrange("p (b e) -> p b e", b=NB)

        raws = src_raw, type_raw, dst_raw = [as_blocks(room[n].bitcast(I32)) for n in range(3)]
        src_f, src_scaled, to_msg_f, dst_f = (as_blocks(room[n]) for n in (3, 0, 1, 2))

        psum = ctx.enter_context(nc.psum_tensor("psum", [P, 8, 512], F32))
        bank = [psum[:, n] for n in range(8)]

        s_pad = sem("s_pad")
        s_lists = sem("s_lists")
        s_float = sem("s_float")
        s_const = sem("s_const")
        s_iota = sem("s_iota")
        s_ident = sem("s_ident")
        s_weights = sem("s_weights")
        s_eps_in = sem("s_eps_in")
        s_eps = sem("s_eps")
        s_listT = sem("s_listT")
        s_listC = sem("s_listC")
        s_base = sem("s_base")
        s_base_c = sem("s_base_c")
        s_local = sem("s_local")
        s_viol = sem("s_viol")
        s_max = sem("s_max")
        s_maxT = sem("s_maxT")
        s_flag = sem("s_flag")
        s_xin = [sem(f"s_xin{n}") for n in range(XS)]
        s_stats = sem("s_stats")
        s_mv = sem("s_mv")
        s_std = sem("s_std")
        s_rstd = sem("s_rstd")
        s_shift = sem("s_shift")
        s_h0 = sem("s_h0")
        s_h0t = sem("s_h0t")
        s_self = [sem(f"s_self{n}") for n in range(C)]
        s_h0st = [sem(f"s_h0st{n}") for n in range(2)]
        s_free = [sem(f"s_free{n}") for n in range(SLOTS)]
        s_idx = [sem(f"s_idx{n}") for n in range(SLOTS)]
        s_rows = [sem(f"s_rows{n}") for n in range(SLOTS)]
        s_onehot = sem("s_onehot")
        s_group = sem("s_group")
        s_added = sem("s_added")
        s_window = sem("s_window")
        s_sums = sem("s_sums")
        s_plan = sem("s_plan")
        s_x = sem("s_x")
        s_y1 = sem("s_y1")
        s_hid = sem("s_hid")
        s_zero = sem("s_zero")
        s_y2 = sem("s_y2")
        s_xb = sem("s_xb")
        s_x1 = sem("s_x1")
        s_x1b = sem("s_x1b")
        s_stats3 = sem("s_stats3")
        s_mv3 = sem("s_mv3")
        s_std3 = sem("s_std3")
        s_rstd3 = sem("s_rstd3")
        s_shift3 = sem("s_shift3")
        s_h1 = sem("s_h1")
        s_h1tp = sem("s_h1tp")
        s_h1t = sem("s_h1t")
        s_msg = [sem(f"s_msg{n}") for n in range(NCH)]
        s_msgc = [sem(f"s_msgc{n}") for n in range(NCH)]
        s_loop = sem("s_loop")
        s_rest = sem("s_rest")
        s_msgst = sem("s_msgst")
        s_restst = sem("s_restst")
        s_rin = sem("s_rin")
        s_fin = sem("s_fin")
        s_fint = sem("s_fint")
        s_out = sem("s_out")
        s_outst = sem("s_outst")
        s_pass = {e: sem(f"s_pass_{e}") for e in ("pool", "act", "dve")}

        set_rows = "(t p) d -> p t d"
        block = ctx.enter_context(nc.Block())

        def next_tile(eng, g):
            return eng.value_load(tile_i[0:1, bass.ds(g + 1, 1)], min_val=0, max_val=EARLY)

        def tiles_of(i, b):
            return KT - PADDED if isinstance(i, int) and i == ROUNDS - 1 and b == SLOTS - 1 else KT

        def set_of(rows_ap, n):
            return rows_ap[bass.ds(n * ST * P, ST * P), :].rearrange(set_rows, p=P)

        @block.sync
        def _(sp):
            for n in range(XS):
                sp.dma_start(xin[:, n], set_of(x, n)).then_inc(s_xin[n], 16)
            sp.dma_start(eps1[:], eps.partition_broadcast(P)).then_inc(s_eps_in, 16)
            sp.wait_ge(s_pad, 1)
            for raw, flat in zip(raws, (src, edge_type, dst)):
                for b, m in ((0, GB), (1, GB - 1)):
                    g = GB * b
                    sp.dma_start(raw[0:m, b, :],
                                 flat[g * GE:(g + m) * GE].rearrange("(g e) -> g e", e=GE)).then_inc(s_lists, 16)
                tiles = raw[GB - 1:GB, 1, :].rearrange("g (p k) -> g k p", k=KT)
                for k in range(WHOLE + 1):
                    a = (NG - 1) * GE + k * P
                    z = min(a + P, E)
                    sp.dma_start(tiles[:, k, 0:z - a], flat[a:z].rearrange("(g p) -> g p", g=1),
                                 allow_slow_non_contiguous=True).then_inc(s_lists, 16)

            def h0_set(n, s):
                sp.wait_ge(s_h0, n + 1)
                if isinstance(n, int) and n == SETS:
                    for a, z in ((0, SPLIT), (SPLIT, LEFT)):
                        sp.dma_start(h0_rows[LAST + a:LAST + z, :], h_out[a:z, s % 2, 0]).then_inc(s_h0st[s % 2], 16)
                else:
                    sp.dma_start(set_of(h0_rows, n), h_out[:, s % 2]).then_inc(s_h0st[s % 2], 16)

            with sp.Fori(0, TURNS - 1) as i:
                for s in range(XS):
                    h0_set(XS * i + s, s)
                    sp.dma_start(xin[:, s], set_of(x, XS * i + s + XS)).then_inc(s_xin[s], 16)
            h0_set(SETS - XS, 0)
            sp.dma_start(xin[0:LEFT, 0, 0], x[LAST:N, :]).then_inc(s_xin[0], 16)
            for s in range(1, XS + 1):
                h0_set(SETS - XS + s, s)

            def feed(layer):
                with sp.Fori(0, ROUNDS) as i:
                    for b in range(SLOTS):
                        sp.wait_ge(s_free[b], i + (layer * ROUNDS + 1))
                        sp.dma_start(idx[:, b], idx_all[:, layer, bass.ds(SLOTS * i + b, 1), :].rearrange(
                            "p g k -> p (g k)")).then_inc(s_idx[b], 16)

            sp.wait_ge(s_listC, LIST_BANKS)
            feed(0)
            sp.wait_ge(s_listC, 3 * LIST_BANKS)
            feed(1)

        @block.gpsimd
        def _(pool):
            nc.gpsimd.iota(iota_i[:], pattern=[[1, P]], base=0, channel_multiplier=0)
            nc.gpsimd.iota(part_i[:], pattern=[[0, 1]], base=0, channel_multiplier=1).then_inc(s_const, 1)
            pool.wait_ge(s_lists, 16 * 3 * (NB + WHOLE + 1))
            nc.gpsimd.tensor_copy(src_f, src_raw).then_inc(s_float, 1)
            nc.gpsimd.tensor_copy(dst_f, dst_raw).then_inc(s_float, 1)
            pool.wait_ge(s_float, 1)
            nc.gpsimd.tensor_scalar(src_scaled, src_f, float(R), None, ALU.mult).then_inc(s_float, 1)
            nc.gpsimd.tensor_copy(to_msg_f, type_raw).then_inc(s_float, 1)
            pool.wait_ge(s_float, 4)
            nc.gpsimd.tensor_tensor(to_msg_f, to_msg_f, src_scaled, ALU.add).then_inc(s_float, 1)

            def gather(layer, table):
                def groups(i):
                    for b in range(SLOTS):
                        pool.wait_ge(s_idx[b], 16 * i + 16 * (layer * ROUNDS + 1))
                        pool.sem_inc(s_pass["pool"], 1)
                        for k in range(tiles_of(i, b)):
                            pool.indirect_dma_start(
                                out=rows[:, b, k], out_offset=None, in_=table,
                                in_offset=bass.IndirectOffsetOnAxis(ap=idx[:, b, k:k + 1], axis=0),
                            ).then_inc(s_rows[b], 16)

                with pool.Fori(0, ROUNDS - 1) as i:
                    groups(i)
                groups(ROUNDS - 1)

            pool.wait_ge(s_h0st[0], 16 * (SETS // 2 + 2))
            pool.wait_ge(s_h0st[1], 16 * (SETS // 2))
            gather(0, h0_rows)
            pool.wait_ge(s_msgst, 32 * (NT + 1))
            gather(1, msg_table)

        @block.scalar
        def _(act):
            def std_set(n, s, tiles):
                act.wait_ge(s_mv, n + 1)
                nc.scalar.activation(std[:, s % 2, 0:tiles], meanvar[:, s % 2, 0:tiles, 1], ACT.Sqrt,
                                     bias=lneps[:]).then_inc(s_std, 1)

            def self_set(n, s, tiles):
                act.wait_ge(s_h0t, n + 1)
                act.sem_inc(s_pass["act"], 1)
                nc.scalar.activation(sums[:, 1, bass.ds(n * (ST * P), tiles * P)],
                                     bank[2 * (s % 2) + 1][:, 0:tiles * P], ACT.Copy, scale=eps1[:]
                                     ).then_inc(s_self[1], 1)

            def h0_set(n, s, stores, tiles):
                act.wait_ge(s_shift, n + 1)
                if later(n, 2):
                    act.wait_ge(s_h0t, n - 1)
                    act.wait_ge(s_h0st[s % 2], 16 * stores)
                for t in range(tiles):
                    last = nc.scalar.activation(h_out[:, s % 2, t], xin[:, s, t], ACT.Relu,
                                                bias=shift[:, s % 2, t:t + 1], scale=rstd[:, s % 2, t:t + 1])
                last.then_inc(s_h0, 1)

            def set_step(n, s, stores, tiles):
                if tiles == ST:
                    std_set(n + 1, s + 1, ST)
                h0_set(n, s, stores, tiles)
                if later(n, 1):
                    self_set(n - 1, s - 1, ST)

            def lists(a):
                for n in range(LIST_BANKS * a, LIST_BANKS * (a + 1)):
                    b, h = n // 2 % NB, n % 2
                    act.wait_ge(s_listT, n + 1)
                    to = (idx_all[:, 0], dst_all[:], idx_all[:, 1])[a]
                    nc.scalar.copy(to[:, b * GB:(b + 1) * GB, 4 * h:4 * h + 4].rearrange("p g k -> p k g"),
                                   bank[4 + n % 4][:, 0:4 * GB].rearrange("p (k g) -> p k g", k=4)
                                   ).then_inc(s_listC, 1)

            act.wait_ge(s_iota, 1)
            nc.scalar.activation(std[:, 1, ST - 1:ST], lneps[:], ACT.Sqrt)
            act.wait_ge(s_eps, 1)
            std_set(0, 0, ST)
            for s in range(XS):
                set_step(s, s, s // 2, ST)
            lists(0)
            with act.Fori(1, TURNS) as i:
                for s in range(XS):
                    set_step(XS * i + s, s, XS // 2 * i + s // 2, ST)
            set_step(SETS, 0, SETS // 2, 1)
            self_set(SETS, 0, 1)
            lists(1)
            lists(2)

            for to, of in ((b2_r[:], b2.partition_broadcast(P)),
                           (bias_r[:], rel_bias.partition_broadcast(P)),
                           (w1[:], W1.rearrange("(k p) d -> p k d", p=P)),
                           (w2[:], W2.rearrange("(k p) d -> p k d", p=P)),
                           (wloop[:], Wloop.rearrange("(k p) d -> p k d", p=P)),
                           (wrel[:, 0], Wrel[:, 0:P].rearrange("r p d -> p r d")),
                           (wrel[:, 1], Wrel[:, P:D].rearrange("r p d -> p r d"))):
                act.dma_start(to, of).then_inc(s_weights, 16)
            act.dma_start(b1_c[:], b1.rearrange("(o p) -> p o", p=P), allow_slow_non_contiguous=True
                          ).then_inc(s_weights, 16)
            act.wait_ge(s_weights, 16 * NCONST)
            act.wait_ge(s_plan, PLAN)
            early = act.value_load(tile_i[0:1, NG + 1:NG + 2], min_val=0, max_val=EARLY)
            act.dma_start(x_in[:], x[0:P, :]).then_inc(s_x, 16)

            def tile_of(rows_ap, j):
                return rows_ap[bass.ds(j * P, P), :]

            def messages(j, n):
                act.wait_ge(s_msg[n], j + 1)
                nc.scalar.copy(msg[:, 512 * n:512 * (n + 1)], bank[MSG_BANK[n]]).then_inc(s_msgc[n], 1)

            def dense(j, g, done):
                act.wait_ge(s_y1, j + 1)
                for o in range(C):
                    last = nc.scalar.activation(hidden[:, o], bank[2][:, o * P:(o + 1) * P], ACT.Relu,
                                                bias=b1_c[:, o:o + 1])
                last.then_inc(s_hid, 1)
                nc.scalar.copy(sums[:, :, bass.ds(j * P, P)], zeros[:]).then_inc(s_zero, 1)
                act.wait_ge(s_mv3, j + 1)
                nc.scalar.activation(std[:, 0, 0:1], meanvar[:, 0, 0, 1:2], ACT.Sqrt,
                                     bias=lneps[:]).then_inc(s_std3, 1)
                act.wait_ge(s_shift3, j + 1)
                nc.scalar.activation(h1[:], x1[:], ACT.Relu, bias=shift[:, 0, 0:1], scale=rstd[:, 0, 0:1]
                                     ).then_inc(s_h1, 1)
                act.wait_ge(s_h1tp, j + 1)
                nc.scalar.copy(h1t[:], bank[3][:, 0:C * P].rearrange("p (c n) -> p c n", c=C)
                               ).then_inc(s_h1t, 1)
                act.wait_ge(s_xb, j + 1)
                act.sem_inc(s_pass["act"], 1)
                with act.If(j < NT - 2):
                    act.dma_start(x_in[:], tile_of(x, nc.s_assert_within(
                        j + 1, 1, NT - 2))).then_inc(s_x, 16)
                with act.Else():
                    act.dma_start(x_in[0:LEFT], x[LAST:N, :]).then_inc(s_x, 16)
                act.wait_ge(s_msgst, 32 * j + 32)
                for n in range(0, NCH, 2):
                    messages(j, n)
                    for m in (n, n + 1):
                        act.wait_ge(s_msgc[m], j + 2)
                    act.dma_start(tile_of(msg_rows, j)[:, 512 * n:512 * (n + 2)], msg[:, 512 * n:512 * (n + 2)]
                                  ).then_inc(s_msgst, 16)
                act.wait_ge(s_rest, j + 2)
                act.dma_start(tile_of(rest_rows, j), rest[:]).then_inc(s_restst, 16)

            def finish(j, g, done):
                if g is not None:
                    act.wait_ge(s_added, g + (done + FREE_BANKS))
                act.sem_inc(s_pass["act"], 1)
                nc.scalar.copy(turned[:], sums[:, :, bass.ds(j * P, P)]).then_inc(s_fin, 1)
                act.wait_ge(s_out, j + 2)
                act.sem_inc(s_pass["act"], 1)
                with act.If(j < NT - 1):
                    whole = nc.s_assert_within(j, 0, NT - 2)
                    act.dma_start(tile_of(out, whole), out_sb[:]).then_inc(s_outst, 16)
                    act.dma_start(rest[:], tile_of(rest_rows, whole + 1)).then_inc(s_rin, 16)
                with act.Else():
                    for a, z in ((0, SPLIT), (SPLIT, LEFT)):
                        act.dma_start(out[LAST + a:LAST + z, :], out_sb[a:z]).then_inc(s_outst, 16)

            def tiles(layer, work):
                with act.Fori(0, ROUNDS) as i:
                    for b in range(SLOTS):
                        g = SLOTS * i + b
                        j, then = next_tile(act, g), next_tile(act, g + 1)
                        with act.If(then > j):
                            work(j, g, layer * NG)
                act.wait_ge(s_sums, layer + 1)
                with act.Fori(early, NT) as j:
                    work(j, None, 0)

            tiles(0, dense)
            act.wait_ge(s_x, 16 * (NT + 1))
            act.wait_ge(s_restst, 16 * (NT + 1))
            act.dma_start(rest[:], rest_rows[0:P, :]).then_inc(s_rin, 16)
            tiles(1, finish)
            act.wait_ge(s_outst, 16 * (NT + 2))

        @block.vector
        def _(dve):
            def stage_in(i, n, s, tiles):
                dve.wait_ge(s_xin[s], 16 * (i + 1))
                for t in range(tiles):
                    last = nc.vector.bn_stats(stats[:, s % 2, t], xin[:, s, t])
                last.then_inc(s_stats, 1)
                dve.wait_ge(s_stats, n + 1)
                dve.sem_inc(s_pass["dve"], 1)
                for t in range(tiles):
                    last = nc.vector.bn_aggr(meanvar[:, s % 2, t], stats[:, s % 2, t])
                last.then_inc(s_mv, 1)

            def stage_norm(n, s, tiles):
                s %= 2
                dve.wait_ge(s_std, n + 1)
                nc.vector.reciprocal(rstd[:, s, 0:tiles], std[:, s, 0:tiles]).then_inc(s_rstd, 1)
                dve.wait_ge(s_rstd, n + 1)
                nc.vector.scalar_tensor_tensor(out=shift[:, s, 0:tiles], in0=meanvar[:, s, 0:tiles, 0],
                                               scalar=-1.0, in1=rstd[:, s, 0:tiles],
                                               op0=ALU.mult, op1=ALU.mult).then_inc(s_shift, 1)

            def stage_self(n, s, tiles):
                dve.wait_ge(s_h0t, n + 1)
                nc.vector.tensor_scalar(sums[:, 0, bass.ds(n * (ST * P), tiles * P)],
                                        bank[2 * (s % 2)][:, 0:tiles * P], eps1[:], None, ALU.mult
                                        ).then_inc(s_self[0], 1)

            for raw, pad in zip(raws, (0, 0, NOWHERE)):
                last = nc.vector.memset(raw[PAD_P:GB, 1], pad)
            last.then_inc(s_pad, 1)
            nc.vector.memset(lneps[:], LN_EPS)
            nc.vector.memset(first[:], 0.0)
            nc.vector.memset(zeros[:], 0.0)
            nc.vector.memset(ones[:], 1.0)
            nc.vector.memset(done_f[:], 0.0)
            nc.vector.memset(sums[:, :, N:ACC], 0.0).then_inc(s_iota, 1)
            dve.wait_ge(s_const, 1)
            nc.vector.tensor_copy(iota_p[:], iota_i[:])
            nc.vector.tensor_copy(part_f[:], part_i[:]).then_inc(s_iota, 1)
            dve.wait_ge(s_iota, 2)
            nc.vector.memset(first[0:1, :], 1.0)
            nc.vector.tensor_scalar(ident[:], iota_p[:], part_f[:], None, ALU.is_equal).then_inc(s_ident, 1)
            dve.wait_ge(s_eps_in, 16)
            nc.vector.tensor_scalar_add(eps1[:], eps1[:], 1.0).then_inc(s_eps, 1)
            dve.wait_ge(s_eps, 1)

            def set_step(i, n, s):
                stage_in(i + (s + 1) // XS, n + 1, (s + 1) % XS, ST)
                if later(n, 2):
                    stage_self(n - 2, s - 2, ST)
                stage_norm(n + 1, s + 1, ST)

            stage_in(0, 0, 0, ST)
            stage_norm(0, 0, ST)
            for s in range(XS):
                set_step(0, s, s)
            with dve.Fori(1, TURNS) as i:
                for s in range(XS):
                    set_step(i, XS * i + s, s)
            for s in range(2):
                stage_self(SETS - 2 + s, s, ST)
            stage_self(SETS, 0, 1)

            dve.wait_ge(s_base, 1)
            nc.vector.tensor_copy(base_f[:], bank[0][:, 0:NG])
            nc.vector.tensor_copy(base_i[:], bank[0][:, 0:NG]).then_inc(s_base_c, 1)
            dve.wait_ge(s_base_c, 1)
            nc.vector.tensor_tensor(local[:, 0:NG], dst_all[:], base_f[:].unsqueeze(2).broadcast_to([P, NG, KT]),
                                    ALU.subtract).then_inc(s_local, 1)
            dve.wait_ge(s_local, 1)
            mid = onehot[:].rearrange("p q k w -> p (q k w)")[:, 0:NG * KT].rearrange("p (g k) -> p g k", k=KT)
            nc.vector.tensor_scalar(mid, local[:, 0:NG], -(W - 1) / 2, None, ALU.add).then_inc(s_viol, 1)
            dve.wait_ge(s_viol, 1)
            nc.vector.memset(mid[:, NG - 1, WHOLE + 1:KT], 0.0)
            nc.vector.memset(mid[OVER:P, NG - 1, WHOLE:WHOLE + 1], 0.0).then_inc(s_viol, 1)
            dve.wait_ge(s_viol, 2)
            nc.vector.tensor_reduce(check[:, 0:1], mid, axis=AX.XY, op=ALU.max, apply_absolute_value=True
                                    ).then_inc(s_viol, 1)
            nc.vector.tensor_tensor(steps_back[:, 0:NG - 1], base_f[:, 0:NG - 1], base_f[:, 1:NG],
                                    ALU.subtract).then_inc(s_viol, 1)
            dve.wait_ge(s_viol, 4)
            nc.vector.tensor_reduce(check[:, 3:4], steps_back[:, 0:NG - 1], axis=AX.X, op=ALU.max
                                    ).then_inc(s_viol, 1)
            dve.wait_ge(s_viol, 5)
            nc.vector.scalar_tensor_tensor(out=check[:, 0:1], in0=check[:, 3:4], scalar=float(W),
                                           in1=check[:, 0:1], op0=ALU.mult, op1=ALU.max).then_inc(s_max, 1)
            dve.wait_ge(s_maxT, 1)
            nc.vector.tensor_reduce(check[0:1, 1:2], bank[1][0:1, 0:P], axis=AX.X, op=ALU.max).then_inc(s_max, 1)
            dve.wait_ge(s_max, 2)
            nc.vector.tensor_scalar(in_windows[0:1, :], check[0:1, 1:2], W / 2, None, ALU.is_lt).then_inc(s_flag, 1)
            nc.vector.tensor_scalar(ready_i[:], base_i[0:1, :], P.bit_length() - 1, None, ALU.arith_shift_right
                                    ).then_inc(s_plan, 1)
            dve.wait_ge(s_plan, 1)
            nc.vector.tensor_scalar(ready[:], ready_i[:], float(EARLY), None, ALU.min).then_inc(s_plan, 1)
            dve.wait_ge(s_plan, 2)
            dve.wait_ge(s_flag, 1)
            nc.vector.tensor_copy(check[0:1, 2:3], in_windows[0:1, :]).then_inc(s_plan, 1)
            dve.wait_ge(s_plan, 3)
            nc.vector.tensor_scalar(ready[:], ready[:], check[0:1, 2:3], None, ALU.mult).then_inc(s_plan, 1)
            dve.wait_ge(s_plan, 4)
            nc.vector.tensor_tensor_scan(out=done_f[:, 2:NG + 2], data0=ones[:], data1=ready[:], initial=0.0,
                                         op0=ALU.add, op1=ALU.min).then_inc(s_plan, 1)
            dve.wait_ge(s_plan, 5)
            nc.vector.tensor_copy(tile_i[:], done_f[:]).then_inc(s_plan, 1)
            dve.wait_ge(s_plan, PLAN)
            windowed = dve.value_load(in_windows[0:1, 0:1], min_val=0, max_val=1)

            def one_hots(q, nodes, dests):
                return nc.vector.tensor_tensor(
                    onehot[:, q, :, 0:W], nodes.unsqueeze(1).broadcast_to([P, KT, W]),
                    dests.rearrange("p g k -> p (g k)").unsqueeze(2).broadcast_to([P, KT, W]), ALU.is_equal)

            def group_one_hots(q, g):
                one_hots(q, iota_p[:, 0:W], local[:, bass.ds(g, 1), :]).then_inc(s_onehot, 1)

            def add(q, at):
                cols = sums[:, :, bass.ds(at, W)]
                return nc.vector.tensor_tensor(cols, cols, bank[q][:, 0:C * W].rearrange("p (c w) -> p c w", c=C),
                                               ALU.add)

            early = dve.value_load(tile_i[0:1, NG + 1:NG + 2], min_val=0, max_val=EARLY)

            def accumulate(layer, before, after):
                def groups(i):
                    done = layer * NG
                    j = next_tile(dve, SLOTS * i)
                    for b in range(SLOTS):
                        g, q = SLOTS * i + b, b % 2
                        at = dve.value_load(base_i[0:1, bass.ds(g, 1)], min_val=0, max_val=N - 1)
                        then = next_tile(dve, g + 1)
                        with dve.If(then > j):
                            before(j)
                        dve.wait_ge(s_group, g + (done + 1))
                        dve.sem_inc(s_free[b], 1)
                        dve.wait_ge(s_added, g + (done + FREE_BANKS))
                        add(q, at).then_inc(s_added, 1)
                        if not isinstance(g, int) or g + AHEAD < NG:
                            group_one_hots(q, g + AHEAD)
                        with dve.If(then > j):
                            after(j)
                        j = then

                with dve.If(windowed == 1):
                    for g in range(AHEAD):
                        group_one_hots(g, g)
                    with dve.Fori(0, ROUNDS - 1) as i:
                        groups(i)
                    groups(ROUNDS - 1)
                    dve.wait_ge(s_added, (layer + 1) * NG + FREE_BANKS)
                with dve.Else():
                    done = layer * NG * NW
                    with dve.Fori(0, ROUNDS) as i:
                        for b in range(SLOTS):
                            g = SLOTS * i + b
                            nc.vector.tensor_scalar(window[:], iota_p[:, 0:W], -float(W), None, ALU.add
                                                    ).then_inc(s_window, 1)
                            with dve.Fori(0, NW) as w:
                                n = g * NW + w
                                dve.wait_ge(s_window, n + g + (layer * NG * (NW + 1) + 1))
                                nc.vector.tensor_scalar(window[:], window[:], float(W), None, ALU.add
                                                        ).then_inc(s_window, 1)
                                dve.wait_ge(s_window, n + g + (layer * NG * (NW + 1) + 2))
                                one_hots(0, window[:], dst_all[:, bass.ds(g, 1), :]).then_inc(s_onehot, 1)
                                dve.wait_ge(s_group, n + (done + 1))
                                dve.wait_ge(s_added, n + (done + FREE_BANKS))
                                add(0, w * W).then_inc(s_added, 1)
                            dve.sem_inc(s_free[b], 1)
                    dve.wait_ge(s_added, done + NG * NW + FREE_BANKS)
                dve.sem_inc(s_sums, 1)
                with dve.Fori(early, NT) as j:
                    before(j)
                    after(j)

            for c in range(C):
                dve.wait_ge(s_self[c], SETS + 1)
            dve.sem_inc(s_added, FREE_BANKS)

            dve.wait_ge(s_weights, 16 * NCONST)

            def dense_before(j):
                dve.wait_ge(s_x, 16 * j + 16)
                nc.vector.tensor_tensor(x_b2[:], x_in[:], b2_r[:], ALU.add).then_inc(s_xb, 1)
                dve.wait_ge(s_xb, j + 1)
                dve.wait_ge(s_y2, j + 1)
                nc.vector.tensor_tensor(x1[:], x_b2[:], bank[2][:, C * P:C * P + D], ALU.add).then_inc(s_x1, 1)
                dve.wait_ge(s_x1, j + 1)
                nc.vector.bn_stats(stats[:, 0, 0], x1[:]).then_inc(s_stats3, 1)
                dve.wait_ge(s_stats3, j + 1)
                dve.sem_inc(s_pass["dve"], 1)
                nc.vector.bn_aggr(meanvar[:, 0, 0], stats[:, 0, 0]).then_inc(s_mv3, 1)
                dve.wait_ge(s_std3, j + 1)
                nc.vector.reciprocal(rstd[:, 0, 0:1], std[:, 0, 0:1]).then_inc(s_rstd3, 1)
                dve.wait_ge(s_rstd3, j + 1)
                nc.vector.scalar_tensor_tensor(out=shift[:, 0, 0:1], in0=meanvar[:, 0, 0, 0:1], scalar=-1.0,
                                               in1=rstd[:, 0, 0:1], op0=ALU.mult, op1=ALU.mult
                                               ).then_inc(s_shift3, 1)
                nc.vector.tensor_tensor(x1_bias[:], x1[:], bias_r[:], ALU.add).then_inc(s_x1b, 1)

            def messages(j, n):
                dve.wait_ge(s_msg[n], j + 1)
                nc.vector.tensor_copy(msg[:, 512 * n:512 * (n + 1)], bank[MSG_BANK[n]]).then_inc(s_msgc[n], 1)

            def dense_after(j):
                dve.wait_ge(s_msgst, 32 * j + 32)
                messages(j, 1)
                messages(j, 3)
                dve.wait_ge(s_x1b, j + 1)
                dve.wait_ge(s_restst, 16 * j + 16)
                dve.wait_ge(s_loop, j + 1)
                nc.vector.scalar_tensor_tensor(out=rest[:], in0=bank[3][:, C * P:C * P + D], scalar=HALF,
                                               in1=x1_bias[:], op0=ALU.mult, op1=ALU.add).then_inc(s_rest, 1)

            accumulate(0, dense_before, dense_after)

            def finish(j):
                dve.wait_ge(s_rin, 16 * j + 16)
                dve.wait_ge(s_outst, 16 * j + 16)
                dve.wait_ge(s_fint, j + 1)
                nc.vector.scalar_tensor_tensor(out=out_sb[:], in0=bank[3][:, 0:D], scalar=HALF,
                                               in1=rest[:], op0=ALU.mult, op1=ALU.add).then_inc(s_out, 1)

            dve.wait_ge(s_zero, NT)
            accumulate(1, lambda j: None, finish)

        @block.tensor
        def _(pe):
            for b in range(SLOTS):
                pe.sem_inc(s_free[b], 1)
            for s in (s_rest, s_out, *s_msgc):
                pe.sem_inc(s, 1)
            for s in (s_restst, s_outst):
                pe.sem_inc(s, 16)
            pe.sem_inc(s_msgst, 32)
            pe.wait_ge(s_ident, 1)

            def turn_h0(n, s, tiles):
                s %= 2
                pe.wait_ge(s_h0, n + 1)
                if later(n, 2):
                    for c in range(C):
                        pe.wait_ge(s_self[c], n - 1)
                for t in range(tiles):
                    for c in range(C):
                        last = nc.tensor.transpose(bank[2 * s + c][:, t * P:(t + 1) * P],
                                                   h_out[:, s, t, c * P:(c + 1) * P], ident[:])
                last.then_inc(s_h0t, 1)

            def lists(a, flat, ready):
                pe.wait_ge(s_float, ready)
                for n in range(LIST_BANKS * a, LIST_BANKS * (a + 1)):
                    b, h = n // 2 % NB, n % 2
                    if a:
                        pe.wait_ge(s_listC, n - LIST_BANKS + 1)
                    for k in range(4):
                        last = nc.tensor.transpose(bank[4 + n % 4][:, k * GB:(k + 1) * GB],
                                                   flat[0:GB, b, 4 * h + k:GE:KT], ident[0:GB, 0:GB])
                    last.then_inc(s_listT, 1)

            for s in range(XS):
                turn_h0(s, s, ST)
            lists(0, src_f, 1)
            with pe.Fori(1, TURNS) as i:
                for s in range(XS):
                    turn_h0(XS * i + s, s, ST)
            turn_h0(SETS, 0, 1)
            lists(1, dst_f, 2)
            lists(2, to_msg_f, 5)
            pe.wait_ge(s_listC, 2 * LIST_BANKS)
            for c in range(C):
                pe.wait_ge(s_self[c], SETS + 1)
            nc.tensor.matmul(bank[0][:, 0:NG], first[:], dst_all[:, :, 0], start=True, stop=True
                             ).then_inc(s_base, 1)
            pe.wait_ge(s_max, 1)
            nc.tensor.matmul(bank[1][0:1, 0:P], check[:, 0:1], ident[:], start=True, stop=True
                             ).then_inc(s_maxT, 1)
            pe.wait_ge(s_plan, PLAN)
            windowed = pe.value_load(in_windows[0:1, 0:1], min_val=0, max_val=1)

            def window_sums(b, q, tiles, part):
                for n in part:
                    c, k = divmod(n, tiles)
                    last = nc.tensor.matmul(bank[q][:, c * W:(c + 1) * W], rows[:, b, k, c * P:(c + 1) * P],
                                            onehot[:, q, k, 0:W], start=k == 0, stop=k == tiles - 1)
                return last

            def gathered(layer, i, b):
                tiles = KT * ROUNDS - (PADDED if b == SLOTS - 1 else 0)
                if tiles_of(i, b) < KT:
                    return 16 * (layer * tiles + tiles)
                return 16 * KT * i + 16 * (layer * tiles + KT)

            early = pe.value_load(tile_i[0:1, NG + 1:NG + 2], min_val=0, max_val=EARLY)

            def accumulate(layer, first, second, turn, third):
                def groups(i):
                    done = layer * NG
                    former, j = next_tile(pe, SLOTS * i - 1), next_tile(pe, SLOTS * i)
                    for b in range(SLOTS):
                        g = SLOTS * i + b
                        then = next_tile(pe, g + 1)
                        tiles = tiles_of(i, b)
                        pe.wait_ge(s_rows[b], gathered(layer, i, b))
                        pe.wait_ge(s_onehot, g + (layer * NG + 1))
                        pe.wait_ge(s_added, g + (done + 1))
                        window_sums(b, b % 2, tiles, range(tiles))
                        with pe.If(j > former):
                            turn(former)
                        with pe.If(then > j):
                            pe.wait_ge(s_added, g + (done + FREE_BANKS))
                            first(j)
                        window_sums(b, b % 2, tiles, range(tiles, tiles * 3 // 2))
                        with pe.If(j > former):
                            third(former)
                        with pe.If(then > j):
                            second(j)
                        window_sums(b, b % 2, tiles, range(tiles * 3 // 2, C * tiles)).then_inc(s_group, 1)
                        former, j = j, then

                def all_windows(i):
                    done = layer * NG * NW
                    for b in range(SLOTS):
                        g = SLOTS * i + b
                        with pe.Fori(0, NW) as w:
                            pe.wait_ge(s_rows[b], gathered(layer, i, b))
                            pe.wait_ge(s_onehot, w + g * NW + (done + 1))
                            pe.wait_ge(s_added, w + g * NW + (done + FREE_BANKS))
                            window_sums(b, 0, tiles_of(i, b), range(C * tiles_of(i, b))).then_inc(s_group, 1)

                with pe.If(windowed == 1):
                    with pe.Fori(0, ROUNDS - 1) as i:
                        groups(i)
                    groups(ROUNDS - 1)
                    last = next_tile(pe, NG - 1)
                    with pe.If(early > last):
                        turn(last)
                        third(last)
                with pe.Else():
                    with pe.Fori(0, ROUNDS - 1) as i:
                        all_windows(i)
                    all_windows(ROUNDS - 1)
                pe.wait_ge(s_sums, layer + 1)
                with pe.Fori(early, NT) as j:
                    first(j)
                    second(j)
                    turn(j)
                    third(j)

            pe.wait_ge(s_weights, 16 * NCONST)
            pe.wait_ge(s_listC, 3 * LIST_BANKS)

            def dense_first(j):
                for o in range(C):
                    for k in range(C):
                        last = nc.tensor.matmul(bank[2][:, o * P:(o + 1) * P], w1[:, k, o * P:(o + 1) * P],
                                                sums[:, k, bass.ds(j * P, P)], start=k == 0, stop=k == C - 1)
                last.then_inc(s_y1, 1)

            def dense_second(j):
                pe.wait_ge(s_hid, j + 1)
                for k in range(C):
                    last = nc.tensor.matmul(bank[2][:, C * P:C * P + D], hidden[:, k], w2[:, k],
                                            start=k == 0, stop=k == C - 1)
                last.then_inc(s_y2, 1)

            def messages(j, n):
                for k in range(C):
                    last = nc.tensor.matmul(bank[MSG_BANK[n]], h1t[:, k],
                                            wrel[:, k, RC * n:RC * (n + 1)].rearrange("p r d -> p (r d)"),
                                            start=k == 0, stop=k == C - 1)
                last.then_inc(s_msg[n], 1)

            def dense_turn(j):
                pe.wait_ge(s_h1, j + 1)
                pe.wait_ge(s_rest, j + 1)
                for c in range(C):
                    last = nc.tensor.transpose(bank[3][:, c * P:(c + 1) * P], h1[:, c * P:(c + 1) * P], ident[:])
                last.then_inc(s_h1tp, 1)

            def dense_third(j):
                pe.wait_ge(s_h1t, j + 1)
                for n in range(NCH):
                    pe.wait_ge(s_msgc[n], j + 1)
                    messages(j, n)
                for k in range(C):
                    last = nc.tensor.matmul(bank[3][:, C * P:C * P + D], h1t[:, k], wloop[:, k],
                                            start=k == 0, stop=k == C - 1)
                last.then_inc(s_loop, 1)

            accumulate(0, dense_first, dense_second, dense_turn, dense_third)

            def nothing(j):
                pass

            def finish(j):
                pe.wait_ge(s_fin, j + 1)
                pe.wait_ge(s_out, j + 1)
                for c in range(C):
                    last = nc.tensor.transpose(bank[3][:, c * P:(c + 1) * P], turned[:, c], ident[:])
                last.then_inc(s_fint, 1)

            pe.wait_ge(s_rest, NT + 1)
            accumulate(1, nothing, finish, nothing, nothing)


_INS = ['x', 'src', 'dst', 'edge_type_8', 'L0_gnn_W1', 'L0_gnn_b1', 'L0_gnn_W2', 'L0_gnn_b2', 'L0_gnn_eps',
        'L1_gnn_weight', 'L1_gnn_h_bias', 'L1_gnn_loop_weight']


def kernel(**inputs):
    import numpy as _np
    import concourse.bacc as _bacc
    from concourse import mybir as _mybir
    from concourse.bass_utils import run_bass_kernel_spmd as _run

    nc = _bacc.Bacc("TRN2", target_bir_lowering=False, num_devices=1)
    arrays, args = {}, []
    for name in _INS:
        a = _np.ascontiguousarray(inputs[name])
        arrays[f"in_{name}_dram"] = a
        args.append(nc.dram_tensor(f"in_{name}_dram", a.shape, _mybir.dt.from_np(a.dtype), kind="ExternalInput").ap())
    out = nc.dram_tensor("out_dram", inputs['x'].shape, _mybir.dt.float32, kind="ExternalOutput").ap()
    gnn_program(nc, *args, out)
    r = _run(nc, [arrays], core_ids=[0])
    return r.results[0]["out_dram"]
```
